# Optimizing a Trainium2 kernel written in Bass

```python
import numpy as np
import jax
import jax.numpy as jnp

def _softmax(x, axis=-1):
    return jax.nn.softmax(x, axis=axis)

def _gelu(x):
    return jax.nn.gelu(x, approximate=True)

def _silu(x):
    return jax.nn.silu(x)

def _sigmoid(x):
    return jax.nn.sigmoid(x)

def _layernorm(x, axis=-1, eps=1e-05):
    m = jnp.mean(x, axis=axis, keepdims=True)
    v = jnp.var(x, axis=axis, keepdims=True)
    return (x - m) / jnp.sqrt(v + eps)

def _scatter_add(tgt, idx, src, axis=0):
    return tgt.at[idx].add(src)

def _segment_sum(src, seg, n):
    return jax.ops.segment_sum(src, seg, n)
kernel_name = 'mk_rec_standalone_d1_rec_r8_ede5ce'

def setup_inputs(seed: int=0):
    np.random.seed(seed)
    _w = jnp.asarray

    def _rec_inputs():
        import jax
        import jax.numpy as jnp
        _rk = jax.random.key(seed)
        r_mask = jax.random.randint(jax.random.fold_in(_rk, 1), (512, 200), 0, 2, jnp.int32)
        return r_mask
    r_mask = _rec_inputs()

    def _L0_rec_setup():
        import jax, jax.numpy as jnp
        import numpy as np
        B, S, D = (512, 200, 64)
        POS_DIM = 2
        H1, H2 = (80, 40)
        NEG_INF = -1000000000.0
        key = jax.random.key(seed)
        ks = jax.random.split(key, 12)
        scale = lambda fan_in: 1.0 / np.sqrt(fan_in)
        return {'sequence_emb': jax.random.normal(ks[0], (B, S, D), dtype=jnp.float32), 'target_emb': jax.random.normal(ks[1], (B, D), dtype=jnp.float32), 'mask': jax.random.randint(ks[2], (B, S), 0, 2, dtype=jnp.int32), 'pos_emb': jax.random.normal(ks[3], (S, POS_DIM), dtype=jnp.float32) * 0.02, 'proj_w': jax.random.normal(ks[4], (D + POS_DIM, D), dtype=jnp.float32) * scale(D + POS_DIM), 'proj_b': jnp.zeros((D,), dtype=jnp.float32), 'w1': jax.random.normal(ks[5], (4 * D, H1), dtype=jnp.float32) * scale(4 * D), 'b1': jnp.zeros((H1,), dtype=jnp.float32), 'w2': jax.random.normal(ks[6], (H1, H2), dtype=jnp.float32) * scale(H1), 'b2': jnp.zeros((H2,), dtype=jnp.float32), 'w3': jax.random.normal(ks[7], (H2, 1), dtype=jnp.float32) * scale(H2), 'b3': jnp.zeros((1,), dtype=jnp.float32)}
    _L0_rec_all = _L0_rec_setup()
    _L0_rec_in = {k: v for k, v in _L0_rec_all.items() if k in ('sequence_emb', 'target_emb', 'pos_emb', 'proj_w', 'proj_b', 'w1', 'b1', 'w2', 'b2', 'w3', 'b3')}
    del _L0_rec_all
    return {'r_mask': r_mask, 'L0_rec_sequence_emb': _L0_rec_in['sequence_emb'], 'L0_rec_target_emb': _L0_rec_in['target_emb'], 'L0_rec_pos_emb': _L0_rec_in['pos_emb'], 'L0_rec_proj_w': _L0_rec_in['proj_w'], 'L0_rec_proj_b': _L0_rec_in['proj_b'], 'L0_rec_w1': _L0_rec_in['w1'], 'L0_rec_b1': _L0_rec_in['b1'], 'L0_rec_w2': _L0_rec_in['w2'], 'L0_rec_b2': _L0_rec_in['b2'], 'L0_rec_w3': _L0_rec_in['w3'], 'L0_rec_b3': _L0_rec_in['b3']}

def reference(r_mask, L0_rec_sequence_emb, L0_rec_target_emb, L0_rec_pos_emb, L0_rec_proj_w, L0_rec_proj_b, L0_rec_w1, L0_rec_b1, L0_rec_w2, L0_rec_b2, L0_rec_w3, L0_rec_b3):
    import jax
    import jax.numpy as jnp

    def _L0_rec_ref(sequence_emb, target_emb, mask, pos_emb, proj_w, proj_b, w1, b1, w2, b2, w3, b3):
        import jax, jax.numpy as jnp
        import numpy as np
        B, S, D = (512, 200, 64)
        POS_DIM = 2
        H1, H2 = (80, 40)
        NEG_INF = -1000000000.0
        tgt = jnp.broadcast_to(target_emb[:, None, :], (B, S, D))
        pos = jnp.broadcast_to(pos_emb[None, :, :], (B, S, POS_DIM))
        tgt = jnp.concatenate([tgt, pos], axis=-1) @ proj_w + proj_b
        din = jnp.concatenate([tgt, sequence_emb, tgt - sequence_emb, tgt * sequence_emb], axis=-1)
        h = jax.nn.sigmoid(din @ w1 + b1)
        h = jax.nn.sigmoid(h @ w2 + b2)
        score = (h @ w3 + b3)[..., 0]
        score = jnp.where(mask == 0, jnp.float32(NEG_INF), score)
        attn = jax.nn.softmax(score, axis=-1)
        return jnp.einsum('bs,bsd->bd', attn, sequence_emb)
    y = _L0_rec_ref(L0_rec_sequence_emb, L0_rec_target_emb, r_mask, L0_rec_pos_emb, L0_rec_proj_w, L0_rec_proj_b, L0_rec_w1, L0_rec_b1, L0_rec_w2, L0_rec_b2, L0_rec_w3, L0_rec_b3)
    return y

_drawn_inputs = setup_inputs


def setup_inputs(seed=0):
    import zlib

    import numpy as np

    out = dict(_drawn_inputs(seed))
    spreads = {'L0_rec_proj_b': (0.0, 2.0), 'L0_rec_b1': (0.0, 2.0), 'L0_rec_b2': (0.0, 2.0)}
    factors = {'L0_rec_pos_emb': 64.0}
    for name, (base, spread) in spreads.items():
        noise = np.random.default_rng([zlib.crc32(name.encode()), seed]).standard_normal(out[name].shape)
        drawn = base * np.exp(spread * noise) if base else spread * noise
        out[name] = jnp.asarray(drawn.astype(out[name].dtype))
    for name, factor in factors.items():
        out[name] = (out[name] * factor).astype(out[name].dtype)
    return out
```

```python
import concourse.bass as bass
from concourse import mybir
from contextlib import ExitStack


def din_attention_program(nc, r_mask, seq, target, pos_emb, proj_w, proj_b, w1, b1, w2, b2, w3, b3, out):
    fp32 = mybir.dt.float32
    i32 = mybir.dt.int32
    ALU = mybir.AluOpType
    ACT = mybir.ActivationFunctionType
    AX = mybir.AxisListType

    B, S, D = seq.shape
    H1, H2 = w2.shape
    POS = pos_emb.shape[1]
    P = 128
    Q = B // P
    BLK = 12
    TRI = 3
    K2 = BLK // TRI
    NBLK = -(-S // BLK)
    LASTN = S - (NBLK - 1) * BLK
    NTRI = -(-S // TRI)
    SPAD = NBLK * BLK
    NEG_INF = -1000000000.0
    LOWEST = -3.0e38

    BODY = 3 * BLK
    LOOP0 = 20
    TURNS = (S - LOOP0) // BODY
    LOOP1 = LOOP0 + TURNS * BODY
    END = S + 34
    SEQ_LAG, PROD_LAG, L1_LAG, ADD_LAG, HID_LAG, L2_LAG, H2_LAG, L3_LAG = 1, 2, 5, 6, 7, 8, 9, 10
    ROWS_LAG, TR_LAG, SOFT_LAG, EXP_LAG, MIX_LAG, SUM_LAG = 22, 23, 24, 26, 26, 28
    NX, NZ, NH, NG = 6, 3, 4, 2
    RING = 3

    seq_v = seq.rearrange("(p q) s d -> p q s d", q=Q)
    mask_v = r_mask.rearrange("(p q) s -> p q s", q=Q)
    tgt_v = target.rearrange("(p q) d -> p q d", q=Q)
    out_v = out.rearrange("(p q) d -> p q d", q=Q)

    ctx = ExitStack()
    with ctx:
        ctx.enter_context(nc.allow_non_contiguous_dma(reason="a few small vectors and the transposed position table"))

        def sb(name, shape, dt=fp32):
            return ctx.enter_context(nc.sbuf_tensor(name, shape, dt))

        def ps(name):
            return ctx.enter_context(nc.psum_tensor(name, [P, 512], fp32))

        def sem(name):
            return ctx.enter_context(nc.semaphore(name))

        seq_sb = [sb(f"seq_sb{r}", [P, Q, BLK, D]) for r in range(RING)]
        mask_i = sb("mask_i", [P, Q, S], i32)
        tgt_sb = sb("tgt_sb", [P, Q, D])
        pos_t = sb("pos_t", [POS, S])
        proj_t2 = sb("proj_t2", [D, 2, D])
        proj_p2 = sb("proj_p2", [POS, 2, D])
        proj_b2 = sb("proj_b2", [P, 1])
        w1a = sb("w1a", [P, H1])
        w1b = sb("w1b", [P, H1])
        w1c = sb("w1c", [P, H1])
        w1d = sb("w1d", [P, H1])
        b1_sb = sb("b1_sb", [H1, 1])
        w2_raw = sb("w2_raw", [H1, H2])
        b2_3 = sb("b2_3", [TRI * H2, 1])
        w3_raw = sb("w3_raw", [H2, 1])
        b3_sb = sb("b3_sb", [BLK, 1])
        ident = sb("ident", [P, P])
        ones = sb("ones", [P, BLK])
        w_add = sb("w_add", [P, 2, H1])
        w_tgt = sb("w_tgt", [P, H1])
        tgt_t = sb("tgt_t", [D, 512])
        T2 = sb("T2", [P, 512])
        P_t = sb("P_t", [D, S])
        w_mul = sb("w_mul", [P, SPAD])
        U = sb("U", [H1, 512])
        V = sb("V", [P, SPAD])
        w2h = sb("w2h", [H1, TRI, H2])
        w2s = sb("w2s", [P, TRI, TRI * H2])
        w3s = sb("w3s", [P, K2 * BLK])
        w3h = sb("w3h", [H2, 1])
        bias2 = sb("bias2", [TRI * H2, 1])
        bias3 = sb("bias3", [BLK, 1])
        keep = sb("keep", [P, Q, S])
        sunk = sb("sunk", [P, Q, S])
        W = [sb(f"W{r}", [P, BLK, H1]) for r in range(RING)]
        Vb = [sb(f"Vb{r}", [P, BLK]) for r in range(RING)]
        X = [sb(f"X{r}", [P, 512]) for r in range(NX)]
        Z = [sb(f"Z{r}", [H1, 512]) for r in range(NZ)]
        Hid = [sb(f"Hid{r}", [P, 512]) for r in range(NH)]
        G = [sb(f"G{r}", [P, 512]) for r in range(NG)]
        rows = sb("rows", [P, 512])
        masked = sb("masked", [P, Q, BLK + 1])
        shifted = sb("shifted", [P, Q, BLK + 1])
        new_max = sb("new_max", [P, Q, 1])
        E = sb("E", [P, Q, BLK + 1])
        mix = sb("mix", [P, Q, BLK + 1, D + 1])
        acc = sb("acc", [P, Q, D + 1])
        inv = sb("inv", [P, Q, 1])
        result = sb("result", [P, Q, D])

        pT = [ps(f"pT{i}") for i in range(2)]
        pL1 = [ps(f"pL1{i}") for i in range(2)]
        pL2 = [ps(f"pL2{i}") for i in range(2)]
        pL3 = ps("pL3")
        pSc = ps("pSc")

        s_seq = [sem(f"seq_loaded{r}") for r in range(RING)]
        s_in = sem("inputs_loaded")
        s_small = sem("small_loaded")
        s_zero = sem("w3_cleared")
        s_set = sem("gpsimd_setup")
        s_pset = sem("tensor_setup")
        s_vset = sem("vector_setup")
        s_aset = sem("scalar_setup")
        s_tr = sem("pair_transposed")
        s_copy = sem("seq_copied")
        s_prod = sem("product_written")
        s_w = sem("weights_built")
        s_wstep = sem("weights_step")
        s_l1 = sem("layer1_done")
        s_add = sem("targets_added")
        s_hid = sem("hidden1_done")
        s_l2 = sem("layer2_done")
        s_g = sem("hidden2_done")
        s_l3 = sem("layer3_done")
        s_rows = sem("rows_copied")
        s_sc = sem("scores_transposed")
        s_read = sem("scores_read")
        s_soft = sem("softmax_step")
        s_exp = sem("exp_done")
        s_mix = sem("mix_done")
        s_sum = sem("block_summed")
        s_fin = sem("final_step")
        s_out = sem("output_stored")

        SOFT = 4
        WSTEP = 2
        MIX = 2 + Q

        FROM_1 = {"scalar": (s_hid, s_exp), "tensor": (s_l1, s_sc), "gpsimd": (s_mix,), "vector": (s_read, s_sum)}

        def start_from_1(eng, name):
            for s in FROM_1[name]:
                eng.sem_inc(s, 1)

        def base(s):
            return 1 if any(s is x for group in FROM_1.values() for x in group) else 0

        def wait(eng, s, first, t, per_turn):
            if isinstance(t, int):
                if first > 0:
                    eng.wait_ge(s, base(s) + first)
            else:
                eng.wait_ge(s, t * per_turn + (base(s) + first))

        def run(eng, slot):
            for tau in range(0, LOOP0):
                slot(tau, 0)
            with eng.Fori(0, TURNS) as t:
                for tau in range(LOOP0, LOOP0 + BODY):
                    slot(tau, t)
            for tau in range(LOOP1, END):
                slot(tau, 0)

        def block_at(tau, lag):
            c, r = divmod(tau - lag, BLK)
            return c if r == 0 and 0 <= c < NBLK else None

        def steps_of(c):
            return LASTN if c == NBLK - 1 else BLK

        block = ctx.enter_context(nc.Block())

        @block.sync
        def _(sp):
            sp.dma_start(tgt_sb[:, :, :], tgt_v).then_inc(s_in, 16)
            sp.dma_start(proj_t2[:, 0, :], proj_w[0:D, :]).then_inc(s_in, 16)
            sp.dma_start(proj_t2[:, 1, :], proj_w[0:D, :]).then_inc(s_in, 16)
            sp.dma_start(seq_sb[0][:, :, :, :], seq_v[:, :, 0:BLK, :]).then_inc(s_seq[0], 16)
            for c in range(1, RING):
                sp.dma_start(seq_sb[c][:, :, :, :], seq_v[:, :, c * BLK:(c + 1) * BLK, :]).then_inc(s_seq[c], 16)
            for c in range(RING, NBLK):
                wait(sp, s_mix, MIX * (c - RING + 1), 0, 0)
                n = steps_of(c)
                sp.dma_start(seq_sb[c % RING][:, :, 0:n, :], seq_v[:, :, c * BLK:c * BLK + n, :])\
                  .then_inc(s_seq[c % RING], 16)
            sp.wait_ge(s_fin, 2)
            sp.dma_start(out_v, result[:, :, :]).then_inc(s_out, 16)
            sp.wait_ge(s_out, 16)

        N_IN = 3 + 2 + 1 + 8 + 4

        @block.scalar
        def _(act):
            start_from_1(act, "scalar")
            act.dma_start(proj_p2[:, 0, :], proj_w[D:D + POS, :]).then_inc(s_in, 16)
            act.dma_start(proj_p2[:, 1, :], proj_w[D:D + POS, :]).then_inc(s_in, 16)
            act.dma_start(pos_t[:, :], pos_emb.rearrange("s j -> j s")).then_inc(s_in, 16)
            for n, w in enumerate((w1a, w1b, w1c, w1d)):
                for h in range(2):
                    act.dma_start(w[h * D:(h + 1) * D, :], w1[n * D:(n + 1) * D, :]).then_inc(s_in, 16)
            act.dma_start(b1_sb[:, :], b1.rearrange("(h a) -> h a", a=1)).then_inc(s_in, 16)
            act.dma_start(w2_raw[:, :], w2).then_inc(s_in, 16)
            act.dma_start(w3_raw[:, :], w3).then_inc(s_in, 16)
            act.dma_start(mask_i[:, :, :], mask_v).then_inc(s_in, 16)
            pb = proj_b.rearrange("(d a) -> d a", a=1)
            for h in range(2):
                act.dma_start(proj_b2[h * D:(h + 1) * D, :], pb).then_inc(s_small, 16)
            for g in range(TRI):
                act.dma_start(b2_3[g * H2:(g + 1) * H2, :], b2.rearrange("(h a) -> h a", a=1)).then_inc(s_small, 16)
            act.dma_start(b3_sb[:, :], b3.rearrange("(a b) -> a b", a=1).to_broadcast([BLK, 1])).then_inc(s_small, 16)
            act.wait_ge(s_zero, 1)
            for g in range(TRI):
                act.dma_start(w3s[g * H2:(g + 1) * H2, g::BLK + TRI], w3.to_broadcast([H2, K2])).then_inc(s_small, 16)
            act.wait_ge(s_pset, 2)
            act.wait_ge(s_small, 16 * 9)
            nc.scalar.activation(T2[:, :], pL1[1][:, :], ACT.Identity, bias=proj_b2[:, 0:1]).then_inc(s_aset, 1)

            def slot(tau, t):
                g = tau - SEQ_LAG
                if 0 <= g < S:
                    h = g % 2 * D
                    if g % 2 == 0:
                        wait(act, s_tr, g // 2 + 1, t, BODY // 2)
                    wait(act, s_l1, g - NX + 1, t, BODY)
                    nc.scalar.activation(X[g % NX][h:h + D, :], pT[g // 2 % 2][h:h + D, :], ACT.Copy)\
                      .then_inc(s_copy, 1)
                g = tau - HID_LAG
                if 0 <= g < S:
                    wait(act, s_add, g + 1, t, BODY)
                    wait(act, s_l2, g - NH + 1, t, BODY)
                    if g % BLK == 0:
                        wait(act, s_w, g // BLK + 1, t, BODY // BLK)
                    nc.scalar.activation(Hid[g % NH][0:H1, :], Z[g % NZ][:, :], ACT.Tanh, scale=0.5,
                                         bias=Vb[g // BLK % RING][0:H1, g % BLK:g % BLK + 1]).then_inc(s_hid, 1)
                g = tau - H2_LAG
                if 0 <= g < S and (g % TRI == TRI - 1 or g == S - 1):
                    k = g // TRI
                    wait(act, s_l2, g + 1, t, BODY)
                    wait(act, s_l3, k - NG + 1, t, BODY // TRI)
                    nc.scalar.activation(G[k % NG][0:TRI * H2, :], pL2[k % 2][0:TRI * H2, :], ACT.Tanh, scale=0.5,
                                         bias=bias2[:, 0:1]).then_inc(s_g, 1)
                c = block_at(tau, ROWS_LAG)
                if c is not None:
                    wait(act, s_l3, min(K2 * (c + 1), NTRI), t, BODY // TRI)
                    wait(act, s_sc, c, t, BODY // BLK)
                    nc.scalar.activation(rows[0:BLK, :], pL3[0:BLK, :], ACT.Identity, bias=bias3[:, 0:1])\
                      .then_inc(s_rows, 1)
                c = block_at(tau, EXP_LAG)
                if c is not None:
                    wait(act, s_soft, SOFT * c + 3, t, SOFT * BODY // BLK)
                    wait(act, s_mix, MIX * c, t, MIX * BODY // BLK)
                    nc.scalar.activation(E[:, :, :], shifted[:, :, :], ACT.Exp).then_inc(s_exp, 1)

            act.wait_ge(s_vset, 8)
            run(act, slot)

        @block.tensor
        def _(pe):
            start_from_1(pe, "tensor")
            pe.wait_ge(s_in, 16 * N_IN)
            pe.wait_ge(s_set, 2)
            for q in range(Q):
                last = nc.tensor.transpose(pL1[0][0:D, q * P:(q + 1) * P], tgt_sb[:, q, :], ident[:, :])
            last.then_inc(s_pset, 1)
            pe.wait_ge(s_vset, 1)
            nc.tensor.matmul(pL1[1][:, :], proj_t2[:, :, :].rearrange("k a m -> k (a m)"), tgt_t[:, :],
                             start=True, stop=True).then_inc(s_pset, 1)
            nc.tensor.matmul(pL2[0][:, 0:S], proj_p2[:, :, :].rearrange("k a m -> k (a m)"), pos_t[:, :],
                             start=True, stop=True).then_inc(s_pset, 1)
            pe.wait_ge(s_vset, 4)
            nc.tensor.matmul(pL2[1][0:H1, 0:S], w_tgt[0:D, :], P_t[:, :], start=True, stop=True).then_inc(s_pset, 1)
            nc.tensor.matmul(pL3[0:TRI * H2, 0:1], w2h[:, :, :].rearrange("k a m -> k (a m)"), ones[0:H1, 0:1],
                             start=True, stop=True).then_inc(s_pset, 1)
            nc.tensor.matmul(pSc[0:BLK, 0:1], ones[0:H2, :], w3h[:, :], start=True, stop=True).then_inc(s_pset, 1)
            pe.wait_ge(s_aset, 1)
            nc.tensor.matmul(pL1[0][0:H1, :], w_tgt[0:D, :], T2[0:D, :], start=True, stop=True).then_inc(s_pset, 1)
            pe.wait_ge(s_vset, 8)

            def slot(tau, t):
                if tau % 2 == 0 and tau < S:
                    p, c, i = tau // 2, tau // BLK, tau % BLK
                    if i == 0:
                        wait(pe, s_seq[c % RING], 16 * (c // RING + 1), t, 16)
                    wait(pe, s_copy, 2 * (p - 2) + 2, t, BODY)
                    for q in range(Q):
                        last = nc.tensor.transpose(
                            pT[p % 2][:, q * P:(q + 1) * P],
                            seq_sb[c % RING][:, q, i:i + 2, :].rearrange("p s d -> p (s d)"), ident[:, :])
                    last.then_inc(s_tr, 1)
                g = tau - L2_LAG
                if 0 <= g < S:
                    k, j = divmod(g, TRI)
                    wait(pe, s_hid, g + 1, t, BODY)
                    if j == 0:
                        wait(pe, s_g, k - 1, t, BODY // TRI)
                    nc.tensor.matmul(pL2[k % 2][0:TRI * H2, :], w2s[:, j, :], Hid[g % NH][:, :], start=(j == 0),
                                     stop=(j == TRI - 1 or g == S - 1)).then_inc(s_l2, 1)
                g = tau - L1_LAG
                if 0 <= g < S:
                    if g % BLK == 0:
                        wait(pe, s_w, g // BLK + 1, t, BODY // BLK)
                    wait(pe, s_prod, g + 1, t, BODY)
                    wait(pe, s_add, g - 1, t, BODY)
                    nc.tensor.matmul(pL1[g % 2][0:H1, :], W[g // BLK % RING][:, g % BLK, :], X[g % NX][:, :],
                                     start=True, stop=True).then_inc(s_l1, 1)
                g = tau - L3_LAG
                if 0 <= g < S and (g % TRI == TRI - 1 or g == S - 1):
                    k = g // TRI
                    j = k % K2
                    wait(pe, s_g, k + 1, t, BODY // TRI)
                    if j == 0:
                        wait(pe, s_rows, k // K2, t, BODY // BLK)
                    nc.tensor.matmul(pL3[0:BLK, :], w3s[:, j * BLK:(j + 1) * BLK], G[k % NG][:, :], start=(j == 0),
                                     stop=(j == K2 - 1 or g == S - 1)).then_inc(s_l3, 1)
                c = block_at(tau, TR_LAG)
                if c is not None:
                    wait(pe, s_rows, c + 1, t, BODY // BLK)
                    wait(pe, s_read, c, t, BODY // BLK)
                    for q in range(Q):
                        last = nc.tensor.transpose(pSc[:, q * P:(q + 1) * P], rows[:, q * P:(q + 1) * P], ident[:, :])
                    last.then_inc(s_sc, 1)

            run(pe, slot)

        @block.gpsimd
        def _(pool):
            start_from_1(pool, "gpsimd")
            nc.gpsimd.memset(w3s[:, :], 0.0).then_inc(s_zero, 1)
            nc.gpsimd.memset(ident[:, :], 0.0).then_inc(s_set, 1)
            nc.gpsimd.memset(ones[:, :], 1.0)
            pool.wait_ge(s_set, 1)
            nc.gpsimd.affine_select(out=ident[:, :], in_=ident[:, :], compare_op=ALU.not_equal, fill=1.0, base=0,
                                    pattern=[[-1, P]], channel_multiplier=1).then_inc(s_set, 1)
            nc.gpsimd.memset(acc[:, :, :], 0.0)
            nc.gpsimd.memset(mix[:, :, :, :], 0.0)
            nc.gpsimd.memset(rows[:, :], 0.0)
            pool.wait_ge(s_in, 16 * N_IN)
            pool.wait_ge(s_vset, 6)

            def weights(c, t):
                r = c % RING
                s0 = c * BLK if isinstance(t, int) else t * BODY + c * BLK
                wait(pool, s_l1, BLK * (c - RING + 1), t, BODY)
                nc.gpsimd.tensor_tensor(W[r][:, :, :], w_mul[:, bass.ds(s0, BLK)].unsqueeze(2).to_broadcast([P, BLK, H1]),
                                        w1d[:, :].unsqueeze(1).to_broadcast([P, BLK, H1]), ALU.mult)\
                  .then_inc(s_wstep, 1)
                wait(pool, s_hid, BLK * (c - RING + 1), t, BODY)
                nc.gpsimd.tensor_copy(Vb[r][:, :], V[:, bass.ds(s0, BLK)]).then_inc(s_wstep, 1)
                wait(pool, s_wstep, WSTEP * (c + 1), t, WSTEP * BODY // BLK)
                pairs = W[r][:, :, :].rearrange("p (s e) h -> p s e h", e=2)
                nc.gpsimd.tensor_tensor(pairs, pairs, w_add[:, :, :].unsqueeze(1).to_broadcast([P, BLK // 2, 2, H1]),
                                        ALU.add).then_inc(s_w, 1)

            def mixing(c, t):
                n = steps_of(c)
                wait(pool, s_exp, c + 1, t, BODY // BLK)
                wait(pool, s_sum, Q * c, t, Q * BODY // BLK)
                e = E[:, :, 0:n].unsqueeze(3)
                nc.gpsimd.tensor_tensor(mix[:, :, BLK, :], acc[:, :, :],
                                        E[:, :, BLK:BLK + 1].to_broadcast([P, Q, D + 1]), ALU.mult)\
                  .then_inc(s_mix, 1)
                nc.gpsimd.tensor_copy(mix[:, :, 0:n, D], E[:, :, 0:n]).then_inc(s_mix, 1)
                for q in range(Q):
                    nc.gpsimd.tensor_tensor(mix[:, q, 0:n, 0:D], seq_sb[c % RING][:, q, 0:n, :],
                                                   E[:, q, 0:n].unsqueeze(2).to_broadcast([P, n, D]), ALU.mult)\
                      .then_inc(s_mix, 1)

            weights(0, 0)
            weights(1, 0)

            def slot(tau, t):
                c = block_at(tau, -4)
                if c is not None and c >= 2:
                    weights(c, t)
                c = block_at(tau, MIX_LAG)
                if c is not None:
                    if c == NBLK - 1:
                        wait(pool, s_sum, Q * c, 0, 0)
                        nc.gpsimd.memset(mix[:, :, LASTN:BLK, :], 0.0)
                    mixing(c, t)

            run(pool, slot)

        @block.vector
        def _(dve):
            start_from_1(dve, "vector")
            dve.wait_ge(s_pset, 1)
            nc.vector.tensor_copy(tgt_t[:, :], pL1[0][0:D, :]).then_inc(s_vset, 1)
            nc.vector.tensor_tensor(w_tgt[:, :], w1a[:, :], w1c[:, :], ALU.add)
            nc.vector.memset(w_add[:, :, :], 0.0).then_inc(s_vset, 1)
            nc.vector.tensor_scalar(w3h[:, :], w3_raw[:, :], 0.5, None, ALU.mult)
            nc.vector.tensor_scalar(w2h[:, :, :], w2_raw[:, :].unsqueeze(1).to_broadcast([H1, TRI, H2]), 0.5, None,
                                    ALU.mult).then_inc(s_vset, 1)
            dve.wait_ge(s_pset, 3)
            nc.vector.memset(w_mul[:, :], 1.0)
            nc.vector.memset(V[:, :], 0.0)
            nc.vector.tensor_copy(P_t[:, :], pL2[0][0:D, 0:S]).then_inc(s_vset, 1)
            nc.vector.memset(w2s[:, :, :], 0.0).then_inc(s_vset, 1)
            dve.wait_ge(s_pset, 4)
            dve.wait_ge(s_vset, 5)
            for h in range(2):
                half = slice(h * D, (h + 1) * D)
                nc.vector.tensor_tensor(w_add[half, h, :], w1b[half, :], w1c[half, :], ALU.subtract)
                nc.vector.tensor_copy(w_mul[half, h:S:2], pL2[0][half, h:S:2])
            nc.vector.tensor_scalar(V[0:H1, 0:S], pL2[1][0:H1, 0:S], b1_sb[:, 0:1], 0.5, ALU.add, ALU.mult)\
              .then_inc(s_vset, 1)
            for g in range(TRI):
                nc.vector.tensor_scalar(w2s[0:H1, g, g * H2:(g + 1) * H2], w2_raw[:, :], 0.5, None, ALU.mult)
            dve.wait_ge(s_small, 16 * 9)
            dve.wait_ge(s_pset, 6)
            nc.vector.tensor_scalar(bias2[:, :], pL3[0:TRI * H2, 0:1], b2_3[:, 0:1], 0.5, ALU.add, ALU.mult)
            nc.vector.tensor_tensor(bias3[:, :], pSc[0:BLK, 0:1], b3_sb[:, :], ALU.add)
            nc.vector.tensor_scalar(w3s[:, :], w3s[:, :], 0.5, None, ALU.mult)
            for hid in Hid:
                nc.vector.memset(hid[D:P, :], 0.0)
            for g in G:
                nc.vector.memset(g[96:P, :], 0.0)
            dve.wait_ge(s_pset, 7)
            nc.vector.tensor_copy(U[:, :], pL1[0][0:H1, :]).then_inc(s_vset, 1)
            nc.vector.tensor_scalar(keep[:, :, :], mask_i[:, :, :], 0.0, None, ALU.not_equal).then_inc(s_vset, 1)
            dve.wait_ge(s_vset, 8)
            nc.vector.tensor_scalar(sunk[:, :, :], keep[:, :, :], 1.0, -NEG_INF, ALU.subtract, ALU.mult)
            nc.vector.memset(masked[:, :, BLK:BLK + 1], LOWEST).then_inc(s_vset, 1)
            dve.wait_ge(s_vset, 9)

            def slot(tau, t):
                g = tau - PROD_LAG
                if 0 <= g < S:
                    h = g % 2 * D
                    wait(dve, s_copy, g + 1, t, BODY)
                    nc.vector.tensor_tensor(X[g % NX][D - h:P - h, :], X[g % NX][h:h + D, :], T2[h:h + D, :],
                                            ALU.mult).then_inc(s_prod, 1)
                g = tau - ADD_LAG
                if 0 <= g < S:
                    wait(dve, s_l1, g + 1, t, BODY)
                    wait(dve, s_hid, g - NZ + 1, t, BODY)
                    nc.vector.tensor_tensor(Z[g % NZ][:, :], pL1[g % 2][0:H1, :], U[:, :], ALU.add)\
                      .then_inc(s_add, 1)

                c = block_at(tau, SOFT_LAG)
                if c is not None:
                    n = steps_of(c)
                    s0 = c * BLK if isinstance(t, int) else t * BODY + c * BLK
                    wait(dve, s_sc, c + 1, t, BODY // BLK)
                    if n < BLK:
                        nc.vector.memset(masked[:, :, n:BLK], LOWEST)
                    nc.vector.tensor_tensor(masked[:, :, 0:n],
                                            pSc[:, :].rearrange("p (q s) -> p q s", q=Q)[:, :, 0:n],
                                            keep[:, :, bass.ds(s0, n)], ALU.mult).then_inc(s_read, 1)
                    wait(dve, s_read, c + 1, t, BODY // BLK)
                    nc.vector.tensor_tensor(masked[:, :, 0:n], masked[:, :, 0:n], sunk[:, :, bass.ds(s0, n)],
                                            ALU.add).then_inc(s_soft, 1)
                c = block_at(tau, SOFT_LAG)
                if c is not None:
                    wait(dve, s_soft, SOFT * c + 1, t, SOFT * BODY // BLK)
                    nc.vector.tensor_reduce(new_max[:, :, :], masked[:, :, :], AX.X, ALU.max).then_inc(s_soft, 1)
                c = block_at(tau, SOFT_LAG + 1)
                if c is not None:
                    wait(dve, s_soft, SOFT * c + 2, t, SOFT * BODY // BLK)
                    wait(dve, s_exp, c, t, BODY // BLK)
                    nc.vector.tensor_tensor(shifted[:, :, :], masked[:, :, :],
                                            new_max[:, :, :].to_broadcast([P, Q, BLK + 1]), ALU.subtract)\
                      .then_inc(s_soft, 1)
                    wait(dve, s_soft, SOFT * c + 3, t, SOFT * BODY // BLK)
                    nc.vector.tensor_copy(masked[:, :, BLK:BLK + 1], new_max[:, :, :]).then_inc(s_soft, 1)
                for q in range(Q):
                    c = block_at(tau, SUM_LAG + q)
                    if c is not None:
                        wait(dve, s_mix, MIX * c + MIX - Q + q + 1, t, MIX * BODY // BLK)
                        nc.vector.tensor_reduce(acc[:, q, :], mix[:, q, :, :].rearrange("p s d -> p d s"), AX.X,
                                                ALU.add).then_inc(s_sum, 1)

            run(dve, slot)
            wait(dve, s_sum, Q * NBLK, 0, 0)
            nc.vector.reciprocal(inv[:, :, :], acc[:, :, D:D + 1]).then_inc(s_fin, 1)
            dve.wait_ge(s_fin, 1)
            nc.vector.tensor_tensor(result[:, :, :], acc[:, :, 0:D], inv[:, :, :].to_broadcast([P, Q, D]), ALU.mult)\
              .then_inc(s_fin, 1)


_INS = ['r_mask', 'L0_rec_sequence_emb', 'L0_rec_target_emb', 'L0_rec_pos_emb', 'L0_rec_proj_w', 'L0_rec_proj_b',
        'L0_rec_w1', 'L0_rec_b1', 'L0_rec_w2', 'L0_rec_b2', 'L0_rec_w3', 'L0_rec_b3']


def kernel(**inputs):
    import numpy as _np
    import concourse.bacc as _bacc
    from concourse import mybir as _mybir
    from concourse.bass_utils import run_bass_kernel_spmd as _run

    nc = _bacc.Bacc("TRN2", target_bir_lowering=False, num_devices=1)
    arrays, args = {}, []
    for name in _INS:
        a = _np.ascontiguousarray(inputs[name])
        arrays[f"in_{name}"] = a
        args.append(nc.dram_tensor(f"in_{name}", a.shape, _mybir.dt.from_np(a.dtype), kind="ExternalInput").ap())
    b, _, d = inputs['L0_rec_sequence_emb'].shape
    out = nc.dram_tensor("out_dram", (b, d), _mybir.dt.float32, kind="ExternalOutput").ap()
    din_attention_program(nc, *args, out)
    r = _run(nc, [arrays], core_ids=[0])
    return r.results[0]["out_dram"]
```

```python
import concourse.bass as bass
from concourse import mybir
from contextlib import ExitStack


def din_attention_program(nc, r_mask, seq, target, pos_emb, proj_w, proj_b, w1, b1, w2, b2, w3, b3, out):
    fp32 = mybir.dt.float32
    fp32r = mybir.dt.float32r
    i32 = mybir.dt.int32
    ALU = mybir.AluOpType
    ACT = mybir.ActivationFunctionType
    AX = mybir.AxisListType

    B, S, D = seq.shape
    H1, H2 = w2.shape
    POS = pos_emb.shape[1]
    P = 128
    Q = B // P
    BLK = 12
    TRI = 3
    K2 = BLK // TRI
    NBLK = -(-S // BLK)
    LASTN = S - (NBLK - 1) * BLK
    NTRI = -(-S // TRI)
    SPAD = NBLK * BLK
    NEG_INF = -1000000000.0
    LOWEST = -3.0e38

    BODY = 3 * BLK
    LOOP0 = 20
    TURNS = (S - LOOP0) // BODY
    LOOP1 = LOOP0 + TURNS * BODY
    END = S + 34
    SEQ_LAG, PROD_LAG, L1_LAG, ADD_LAG, HID_LAG, L2_LAG, H2_LAG, L3_LAG = 1, 2, 5, 6, 7, 8, 9, 11
    ROWS_LAG, TR_LAG, SOFT_LAG, EXP_LAG, MIX_LAG = 23, 24, 25, 27, 27
    SUM_LAG = (29, 30, 31, 31)
    MASK_SLOT = 14
    NX, NZ, NH, NG = 6, 3, 4, 2
    RING = 3

    seq_v = seq.rearrange("(p q) s d -> p q s d", q=Q)
    mask_v = r_mask.rearrange("(p q) s -> p q s", q=Q)
    tgt_v = target.rearrange("(p q) d -> p q d", q=Q)
    out_v = out.rearrange("(p q) d -> p q d", q=Q)

    ctx = ExitStack()
    with ctx:
        ctx.enter_context(nc.allow_non_contiguous_dma(reason="a few small vectors and the transposed position table"))

        def sb(name, shape, dt=fp32):
            return ctx.enter_context(nc.sbuf_tensor(name, shape, dt))

        def ps(name):
            return ctx.enter_context(nc.psum_tensor(name, [P, 512], fp32))

        def sem(name):
            return ctx.enter_context(nc.semaphore(name))

        seq_sb = [sb(f"seq_sb{r}", [P, Q, BLK, D]) for r in range(RING)]
        mask_i = sb("mask_i", [P, Q, S], i32)
        tgt_sb = sb("tgt_sb", [P, Q, D])
        pos_t = sb("pos_t", [POS, S])
        proj_t2 = sb("proj_t2", [D, 2, D])
        proj_p2 = sb("proj_p2", [POS, 2, D])
        proj_b2 = sb("proj_b2", [P, 1])
        w1_sb = sb("w1_sb", [P, 4, H1])
        w1a, w1b, w1c, w1d = (w1_sb[:, n, :] for n in range(4))
        b1_sb = sb("b1_sb", [H1, 1])
        w2_raw = sb("w2_raw", [H1, H2])
        b2_3 = sb("b2_3", [TRI * H2, 1])
        w3_raw = sb("w3_raw", [H2, 1])
        b3_sb = sb("b3_sb", [BLK, 1])
        ident = sb("ident", [P, P])
        ones = sb("ones", [P, BLK])
        w_add = sb("w_add", [P, 2, H1])
        w_tgt = sb("w_tgt", [P, H1])
        tgt_t = sb("tgt_t", [D, 512])
        T2 = sb("T2", [P, 512])
        P_t = sb("P_t", [D, S])
        w_mul = sb("w_mul", [P, SPAD])
        U = sb("U", [H1, 512])
        V = sb("V", [P, SPAD])
        w2h = sb("w2h", [H1, TRI, H2])
        w2s = sb("w2s", [P, TRI, TRI * H2])
        w3s = sb("w3s", [P, K2, BLK])
        w3p = sb("w3p", [P, K2, 2, BLK], fp32r)
        w3h = sb("w3h", [H2, 1])
        bias2 = sb("bias2", [TRI * H2, 1])
        bias3 = sb("bias3", [2 * BLK, 1])
        keep = sb("keep", [P, Q, S])
        sunk = sb("sunk", [P, Q, S])
        W = [sb(f"W{r}", [P, BLK, H1]) for r in range(RING)]
        Vb = [sb(f"Vb{r}", [P, BLK]) for r in range(RING)]
        X = [sb(f"X{r}", [P, 512]) for r in range(NX)]
        Z = [sb(f"Z{r}", [H1, 512]) for r in range(NZ)]
        Hid = [sb(f"Hid{r}", [P, 512]) for r in range(NH)]
        G = [sb(f"G{r}", [P, 512]) for r in range(NG)]
        Ghi = [sb(f"Ghi{r}", [P, 512], fp32r) for r in range(NG)]
        Glo = [sb(f"Glo{r}", [P, 512], fp32r) for r in range(NG)]
        rows = sb("rows", [P, 512])
        masked = sb("masked", [P, Q, BLK + 1])
        shifted = sb("shifted", [P, Q, BLK + 1])
        new_max = sb("new_max", [P, Q, 1])
        E = sb("E", [P, Q, BLK + 1])
        mix = sb("mix", [P, Q, BLK + 1, D + 1])
        acc = sb("acc", [P, Q, D + 1])
        inv = sb("inv", [P, Q, 1])
        result = sb("result", [P, Q, D])

        pT = [ps(f"pT{i}") for i in range(2)]
        pL1 = [ps(f"pL1{i}") for i in range(2)]
        pL2 = [ps(f"pL2{i}") for i in range(2)]
        pL3 = ps("pL3")
        pSc = ps("pSc")

        s_seq = [sem(f"seq_loaded{r}") for r in range(RING)]
        s_in = sem("inputs_loaded")
        s_small = sem("small_loaded")
        s_tiny = sem("small_loaded_by_gpsimd")
        s_mask = sem("mask_loaded")
        s_keep = sem("mask_factors")
        s_zero = sem("w3_cleared")
        s_set = sem("gpsimd_setup")
        s_pset = sem("tensor_setup")
        s_vset = sem("vector_setup")
        s_aset = sem("scalar_setup")
        s_tr = sem("pair_transposed")
        s_copy = sem("seq_copied")
        s_prod = sem("product_written")
        s_w3 = sem("w3_split")
        s_w = sem("weights_built")
        s_wstep = sem("weights_step")
        s_l1 = sem("layer1_done")
        s_add = sem("targets_added")
        s_hid = sem("hidden1_done")
        s_l2 = sem("layer2_done")
        s_g = sem("hidden2_done")
        s_glo = sem("hidden2_split")
        s_l3 = sem("layer3_done")
        s_rows = sem("rows_copied")
        s_sc = sem("scores_transposed")
        s_read = sem("scores_read")
        s_soft = sem("softmax_step")
        s_exp = sem("exp_done")
        s_mix = sem("mix_done")
        s_sum = sem("block_summed")
        s_fin = sem("final_step")
        s_out = sem("output_stored")

        SOFT = 5
        WSTEP = 2
        MIX = 2 + Q

        FROM_1 = {"scalar": (s_hid, s_exp), "tensor": (s_l1, s_sc), "gpsimd": (s_mix,), "vector": (s_read, s_sum)}

        def start_from_1(eng, name):
            for s in FROM_1[name]:
                eng.sem_inc(s, 1)

        def base(s):
            return 1 if any(s is x for group in FROM_1.values() for x in group) else 0

        def wait(eng, s, first, t, per_turn):
            if isinstance(t, int):
                if first > 0:
                    eng.wait_ge(s, base(s) + first)
            else:
                eng.wait_ge(s, t * per_turn + (base(s) + first))

        def run(eng, slot, first=0):
            for tau in range(first, LOOP0):
                slot(tau, 0)
            with eng.Fori(0, TURNS) as t:
                for tau in range(LOOP0, LOOP0 + BODY):
                    slot(tau, t)
            for tau in range(LOOP1, END):
                slot(tau, 0)

        def block_at(tau, lag):
            c, r = divmod(tau - lag, BLK)
            return c if r == 0 and 0 <= c < NBLK else None

        def steps_of(c):
            return LASTN if c == NBLK - 1 else BLK

        N_IN, N_SMALL, N_TINY = 2 + 4, 4, 2 * TRI + 2

        block = ctx.enter_context(nc.Block())

        @block.sync
        def _(sp):
            sp.dma_start(tgt_sb[:, :, :], tgt_v).then_inc(s_in, 16)
            sp.dma_start(proj_t2[:, :, :], proj_w[0:D, :].unsqueeze(1).to_broadcast([D, 2, D])).then_inc(s_in, 16)
            sp.dma_start(seq_sb[0][:, :, :, :], seq_v[:, :, 0:BLK, :]).then_inc(s_seq[0], 16)
            sp.wait_ge(s_small, 16 * N_SMALL)
            sp.wait_ge(s_tiny, 16 * N_TINY)
            sp.dma_start(mask_i[:, :, :], mask_v).then_inc(s_mask, 16)
            for c in range(1, RING):
                sp.dma_start(seq_sb[c][:, :, :, :], seq_v[:, :, c * BLK:(c + 1) * BLK, :]).then_inc(s_seq[c], 16)
            for c in range(RING, NBLK):
                wait(sp, s_mix, MIX * (c - RING + 1), 0, 0)
                n = steps_of(c)
                sp.dma_start(seq_sb[c % RING][:, :, 0:n, :], seq_v[:, :, c * BLK:c * BLK + n, :])\
                  .then_inc(s_seq[c % RING], 16)
            sp.wait_ge(s_fin, 2)
            sp.dma_start(out_v, result[:, :, :]).then_inc(s_out, 16)
            sp.wait_ge(s_out, 16)



        @block.scalar
        def _(act):
            start_from_1(act, "scalar")
            act.dma_start(proj_p2[:, :, :], proj_w[D:D + POS, :].unsqueeze(1).to_broadcast([POS, 2, D])).then_inc(s_in, 16)
            act.dma_start(pos_t[:, :], pos_emb.rearrange("s j -> j s")).then_inc(s_in, 16)
            for h in range(2):
                act.dma_start(w1_sb[h * D:(h + 1) * D, :, :], w1.rearrange("(n d) h -> d n h", d=D)).then_inc(s_in, 16)
            for h in range(2):
                act.dma_start(proj_b2[h * D:(h + 1) * D, :], proj_b.rearrange("(d a) -> d a", a=1))\
                   .then_inc(s_small, 16)
            act.dma_start(b1_sb[:, :], b1.rearrange("(h a) -> h a", a=1)).then_inc(s_small, 16)
            act.dma_start(w2_raw[:, :], w2).then_inc(s_small, 16)
            act.wait_ge(s_pset, 3)
            act.wait_ge(s_small, 16 * N_SMALL)
            nc.scalar.activation(T2[:, :], pL1[1][:, :], ACT.Identity, bias=proj_b2[:, 0:1]).then_inc(s_aset, 1)

            def slot(tau, t):
                g = tau - SEQ_LAG
                if 0 <= g < S:
                    h = g % 2 * D
                    if g % 2 == 0:
                        wait(act, s_tr, g // 2 + 1, t, BODY // 2)
                    wait(act, s_l1, g - NX + 1, t, BODY)
                    nc.scalar.activation(X[g % NX][h:h + D, :], pT[g // 2 % 2][h:h + D, :], ACT.Copy)\
                      .then_inc(s_copy, 1)
                g = tau - HID_LAG
                if 0 <= g < S:
                    wait(act, s_add, g + 1, t, BODY)
                    wait(act, s_l2, g - NH + 1, t, BODY)
                    if g % BLK == 0:
                        wait(act, s_w, g // BLK + 1, t, BODY // BLK)
                    nc.scalar.activation(Hid[g % NH][0:H1, :], Z[g % NZ][:, :], ACT.Tanh, scale=0.5,
                                         bias=Vb[g // BLK % RING][0:H1, g % BLK:g % BLK + 1]).then_inc(s_hid, 1)
                g = tau - H2_LAG
                if 0 <= g < S and (g % TRI == TRI - 1 or g == S - 1):
                    k = g // TRI
                    wait(act, s_l2, g + 1, t, BODY)
                    wait(act, s_l3, k - NG + 1, t, BODY // TRI)
                    for part in (G, Ghi):
                        nc.scalar.activation(part[k % NG][0:TRI * H2, :], pL2[k % 2][0:TRI * H2, :], ACT.Tanh,
                                             scale=0.5, bias=bias2[:, 0:1]).then_inc(s_g, 1)
                c = block_at(tau, ROWS_LAG)
                if c is not None:
                    wait(act, s_l3, min(K2 * (c + 1), NTRI), t, BODY // TRI)
                    wait(act, s_sc, c, t, BODY // BLK)
                    nc.scalar.activation(rows[0:2 * BLK, :], pL3[0:2 * BLK, :], ACT.Identity, bias=bias3[:, 0:1])\
                      .then_inc(s_rows, 1)
                c = block_at(tau, EXP_LAG)
                if c is not None:
                    wait(act, s_soft, SOFT * c + 4, t, SOFT * BODY // BLK)
                    wait(act, s_mix, MIX * c, t, MIX * BODY // BLK)
                    n = steps_of(c) + 1
                    nc.scalar.activation(E[:, :, 0:n], shifted[:, :, 0:n], ACT.Exp).then_inc(s_exp, 1)

            for tau in range(HID_LAG):
                slot(tau, 0)
            act.wait_ge(s_vset, 7)
            act.wait_ge(s_set, 3)
            run(act, slot, HID_LAG)

        @block.tensor
        def _(pe):
            start_from_1(pe, "tensor")
            pe.wait_ge(s_in, 16 * N_IN)
            pe.wait_ge(s_set, 2)
            for q in range(Q):
                last = nc.tensor.transpose(pL1[0][0:D, q * P:(q + 1) * P], tgt_sb[:, q, :], ident[:, :])
            last.then_inc(s_pset, 1)
            nc.tensor.matmul(pL2[0][:, 0:S], proj_p2[:, :, :].rearrange("k a m -> k (a m)"), pos_t[:, :],
                             start=True, stop=True).then_inc(s_pset, 1)
            pe.wait_ge(s_vset, 2)
            nc.tensor.matmul(pL1[1][:, :], proj_t2[:, :, :].rearrange("k a m -> k (a m)"), tgt_t[:, :],
                             start=True, stop=True).then_inc(s_pset, 1)
            pe.wait_ge(s_vset, 3)
            nc.tensor.matmul(pL2[1][0:H1, 0:S], w_tgt[0:D, :], P_t[:, :], start=True, stop=True).then_inc(s_pset, 1)
            pe.wait_ge(s_vset, 6)
            nc.tensor.matmul(pL3[0:TRI * H2, 0:1], w2h[:, :, :].rearrange("k a m -> k (a m)"), ones[0:H1, 0:1],
                             start=True, stop=True).then_inc(s_pset, 1)
            nc.tensor.matmul(pSc[0:BLK, 0:1], ones[0:H2, :], w3h[:, :], start=True, stop=True).then_inc(s_pset, 1)
            def slot(tau, t):
                if tau % 2 == 0 and tau < S:
                    p, c, i = tau // 2, tau // BLK, tau % BLK
                    if i == 0:
                        wait(pe, s_seq[c % RING], 16 * (c // RING + 1), t, 16)
                    wait(pe, s_copy, 2 * (p - 2) + 2, t, BODY)
                    for q in range(Q):
                        last = nc.tensor.transpose(
                            pT[p % 2][:, q * P:(q + 1) * P],
                            seq_sb[c % RING][:, q, i:i + 2, :].rearrange("p s d -> p (s d)"), ident[:, :])
                    last.then_inc(s_tr, 1)
                g = tau - L2_LAG
                if 0 <= g < S:
                    k, j = divmod(g, TRI)
                    wait(pe, s_hid, g + 1, t, BODY)
                    if j == 0:
                        wait(pe, s_g, 2 * (k - 1), t, 2 * BODY // TRI)
                    nc.tensor.matmul(pL2[k % 2][0:TRI * H2, :], w2s[:, j, :], Hid[g % NH][:, :], start=(j == 0),
                                     stop=(j == TRI - 1 or g == S - 1)).then_inc(s_l2, 1)
                g = tau - L1_LAG
                if 0 <= g < S:
                    if g % BLK == 0:
                        wait(pe, s_w, g // BLK + 1, t, BODY // BLK)
                    wait(pe, s_prod, g + 1, t, BODY)
                    wait(pe, s_add, g - 1, t, BODY)
                    nc.tensor.matmul(pL1[g % 2][0:H1, :], W[g // BLK % RING][:, g % BLK, :], X[g % NX][:, :],
                                     start=True, stop=True).then_inc(s_l1, 1)
                g = tau - L3_LAG
                if 0 <= g < S and (g % TRI == TRI - 1 or g == S - 1):
                    k = g // TRI
                    j = k % K2
                    wait(pe, s_glo, k + 1, t, BODY // TRI)
                    if j == 0:
                        wait(pe, s_rows, k // K2, t, BODY // BLK)
                    w = w3p[:, j, :, :].rearrange("k a m -> k (a m)")
                    nc.tensor.matmul(pL3[0:2 * BLK, :], w, Ghi[k % NG][:, :], start=(j == 0), stop=False)
                    nc.tensor.matmul(pL3[0:2 * BLK, :], w, Glo[k % NG][:, :], start=False,
                                     stop=(j == K2 - 1 or g == S - 1)).then_inc(s_l3, 1)
                c = block_at(tau, TR_LAG)
                if c is not None:
                    wait(pe, s_rows, c + 1, t, BODY // BLK)
                    wait(pe, s_read, c, t, BODY // BLK)
                    for q in range(Q):
                        last = nc.tensor.transpose(pSc[:, q * P:(q + 1) * P], rows[:, q * P:(q + 1) * P], ident[:, :])
                    last.then_inc(s_sc, 1)

            for tau in range(4):
                slot(tau, 0)
            pe.wait_ge(s_aset, 1)
            nc.tensor.matmul(pL1[0][0:H1, :], w_tgt[0:D, :], T2[0:D, :], start=True, stop=True).then_inc(s_pset, 1)
            pe.wait_ge(s_vset, 8)
            run(pe, slot, 4)

        @block.gpsimd
        def _(pool):
            start_from_1(pool, "gpsimd")
            nc.gpsimd.memset(w3s[:, :, :], 0.0).then_inc(s_zero, 1)
            nc.gpsimd.memset(ident[:, :], 0.0).then_inc(s_set, 1)
            nc.gpsimd.memset(ones[:, :], 1.0)
            pool.wait_ge(s_set, 1)
            nc.gpsimd.affine_select(out=ident[:, :], in_=ident[:, :], compare_op=ALU.not_equal, fill=1.0, base=0,
                                    pattern=[[-1, P]], channel_multiplier=1).then_inc(s_set, 1)
            pool.wait_ge(s_zero, 1)
            for g in range(TRI):
                pool.dma_start(w3s[g * H2:(g + 1) * H2, :, :].rearrange("h k c -> h (k c)")[:, g::BLK + TRI],
                               w3.to_broadcast([H2, K2])).then_inc(s_tiny, 16)
            pool.dma_start(w3_raw[:, :], w3).then_inc(s_tiny, 16)
            for g in range(TRI):
                pool.dma_start(b2_3[g * H2:(g + 1) * H2, :], b2.rearrange("(h a) -> h a", a=1)).then_inc(s_tiny, 16)
            pool.dma_start(b3_sb[:, :], b3.rearrange("(a b) -> a b", a=1).to_broadcast([BLK, 1])).then_inc(s_tiny, 16)
            nc.gpsimd.memset(acc[:, :, :], 0.0)
            nc.gpsimd.memset(rows[:, :], 0.0)
            for hid in Hid:
                nc.gpsimd.memset(hid[:, :], 0.0)
            for part in G:
                nc.gpsimd.memset(part[:, :], 0.0)
            for part in Ghi:
                last = nc.gpsimd.memset(part[:, :].bitcast(fp32), 0.0)
            last.then_inc(s_set, 1)
            def weights(c, t):
                r = c % RING
                s0 = c * BLK if isinstance(t, int) else t * BODY + c * BLK
                if c == 0:
                    pool.wait_ge(s_vset, 4)
                wait(pool, s_l1, BLK * (c - RING + 1), t, BODY)
                nc.gpsimd.tensor_tensor(W[r][:, :, :], w_mul[:, bass.ds(s0, BLK)].unsqueeze(2).to_broadcast([P, BLK, H1]),
                                        w1d[:, :].unsqueeze(1).to_broadcast([P, BLK, H1]), ALU.mult)\
                  .then_inc(s_wstep, 1)
                if c == 0:
                    pool.wait_ge(s_vset, 5)
                wait(pool, s_hid, BLK * (c - RING + 1), t, BODY)
                nc.gpsimd.tensor_copy(Vb[r][:, :], V[:, bass.ds(s0, BLK)]).then_inc(s_wstep, 1)
                wait(pool, s_wstep, WSTEP * (c + 1), t, WSTEP * BODY // BLK)
                pairs = W[r][:, :, :].rearrange("p (s e) h -> p s e h", e=2)
                nc.gpsimd.tensor_tensor(pairs, pairs, w_add[:, :, :].unsqueeze(1).to_broadcast([P, BLK // 2, 2, H1]),
                                        ALU.add).then_inc(s_w, 1)

            def mixing(c, t):
                n = steps_of(c)
                wait(pool, s_exp, c + 1, t, BODY // BLK)
                wait(pool, s_sum, Q * c, t, Q * BODY // BLK)
                nc.gpsimd.tensor_tensor(mix[:, :, 0, :], acc[:, :, :], E[:, :, 0:1].to_broadcast([P, Q, D + 1]),
                                        ALU.mult).then_inc(s_mix, 1)
                nc.gpsimd.tensor_copy(mix[:, :, 1:n + 1, D], E[:, :, 1:n + 1]).then_inc(s_mix, 1)
                for q in range(Q):
                    nc.gpsimd.tensor_tensor(mix[:, q, 1:n + 1, 0:D], seq_sb[c % RING][:, q, 0:n, :],
                                            E[:, q, 1:n + 1].unsqueeze(2).to_broadcast([P, n, D]), ALU.mult)\
                      .then_inc(s_mix, 1)

            weights(0, 0)
            weights(1, 0)

            def slot(tau, t):
                c = block_at(tau, -4)
                if c is not None and c >= 2:
                    weights(c, t)
                c = block_at(tau, MIX_LAG)
                if c is not None:
                    mixing(c, t)

            run(pool, slot)

        @block.vector
        def _(dve):
            start_from_1(dve, "vector")
            nc.vector.memset(w_add[:, :, :], 0.0)
            nc.vector.memset(w_mul[:, :], 1.0)
            nc.vector.memset(V[:, :], 0.0)
            nc.vector.memset(bias3[:, :], 0.0)
            nc.vector.memset(masked[:, :, 0:1], LOWEST)
            nc.vector.memset(w2s[:, :, :], 0.0).then_inc(s_vset, 1)
            dve.wait_ge(s_in, 16 * N_IN)
            nc.vector.tensor_tensor(w_tgt[:, :], w1a, w1c, ALU.add)
            dve.wait_ge(s_pset, 1)
            nc.vector.tensor_copy(tgt_t[:, :], pL1[0][0:D, :]).then_inc(s_vset, 1)
            dve.wait_ge(s_pset, 2)
            nc.vector.tensor_copy(P_t[:, :], pL2[0][0:D, 0:S]).then_inc(s_vset, 1)
            dve.wait_ge(s_vset, 1)
            for h in range(2):
                half = slice(h * D, (h + 1) * D)
                nc.vector.tensor_tensor(w_add[half, h, :], w1b[half, :], w1c[half, :], ALU.subtract)
                last = nc.vector.tensor_copy(w_mul[half, h:S:2], pL2[0][half, h:S:2])
            last.then_inc(s_vset, 1)
            dve.wait_ge(s_pset, 4)
            dve.wait_ge(s_small, 16 * N_SMALL)
            dve.wait_ge(s_tiny, 16 * N_TINY)
            nc.vector.tensor_scalar(V[0:H1, 0:S], pL2[1][0:H1, 0:S], b1_sb[:, 0:1], 0.5, ALU.add, ALU.mult)\
              .then_inc(s_vset, 1)
            nc.vector.tensor_scalar(w3h[:, :], w3_raw[:, :], 0.5, None, ALU.mult)
            nc.vector.tensor_scalar(w2h[:, :, :], w2_raw[:, :].unsqueeze(1).to_broadcast([H1, TRI, H2]), 0.5, None,
                                    ALU.mult).then_inc(s_vset, 1)
            for g in range(TRI):
                nc.vector.tensor_scalar(w2s[0:H1, g, g * H2:(g + 1) * H2], w2_raw[:, :], 0.5, None, ALU.mult)
            nc.vector.tensor_scalar(w3p[:, :, 0, :], w3s[:, :, :], 0.5, None, ALU.mult).then_inc(s_w3, 1)
            dve.wait_ge(s_w3, 1)
            nc.vector.scalar_tensor_tensor(out=w3p[:, :, 1, :], in0=w3s[:, :, :], scalar=0.5,
                                           in1=w3p[:, :, 0, :].bitcast(fp32), op0=ALU.mult, op1=ALU.subtract)
            dve.wait_ge(s_pset, 6)
            nc.vector.tensor_scalar(bias2[:, :], pL3[0:TRI * H2, 0:1], b2_3[:, 0:1], 0.5, ALU.add, ALU.mult)
            nc.vector.tensor_tensor(bias3[0:BLK, :], pSc[0:BLK, 0:1], b3_sb[:, :], ALU.add).then_inc(s_vset, 1)
            dve.wait_ge(s_pset, 7)
            nc.vector.tensor_copy(U[:, :], pL1[0][0:H1, :]).then_inc(s_vset, 1)
            dve.wait_ge(s_vset, 8)

            def mask_factors():
                dve.wait_ge(s_mask, 16)
                nc.vector.tensor_scalar(keep[:, :, :], mask_i[:, :, :], 0.0, None, ALU.not_equal).then_inc(s_keep, 1)
                dve.wait_ge(s_keep, 1)
                nc.vector.tensor_scalar(sunk[:, :, :], keep[:, :, :], 1.0, -NEG_INF, ALU.subtract, ALU.mult)\
                  .then_inc(s_keep, 1)

            def slot(tau, t):
                if tau == MASK_SLOT:
                    mask_factors()
                g = tau - PROD_LAG
                if 0 <= g < S:
                    h = g % 2 * D
                    wait(dve, s_copy, g + 1, t, BODY)
                    nc.vector.tensor_tensor(X[g % NX][D - h:P - h, :], X[g % NX][h:h + D, :], T2[h:h + D, :],
                                            ALU.mult).then_inc(s_prod, 1)
                g = tau - ADD_LAG
                if 0 <= g < S:
                    wait(dve, s_l1, g + 1, t, BODY)
                    wait(dve, s_hid, g - NZ + 1, t, BODY)
                    nc.vector.tensor_tensor(Z[g % NZ][:, :], pL1[g % 2][0:H1, :], U[:, :], ALU.add)\
                      .then_inc(s_add, 1)

                g = tau - H2_LAG - 1
                if 0 <= g < S and (g % TRI == TRI - 1 or g == S - 1):
                    k = g // TRI
                    wait(dve, s_g, 2 * k + 2, t, 2 * BODY // TRI)
                    wait(dve, s_l3, k - NG + 1, t, BODY // TRI)
                    nc.vector.tensor_tensor(Glo[k % NG][:, :], G[k % NG][:, :], Ghi[k % NG][:, :].bitcast(fp32),
                                            ALU.subtract).then_inc(s_glo, 1)
                c = block_at(tau, SOFT_LAG)
                if c is not None:
                    n = steps_of(c)
                    s0 = c * BLK if isinstance(t, int) else t * BODY + c * BLK
                    wait(dve, s_sc, c + 1, t, BODY // BLK)
                    nc.vector.tensor_reduce(masked[:, :, 1:n + 1], pSc[:, :].rearrange("p (q s) -> p q s", q=Q)
                                            [:, :, 0:2 * BLK].rearrange("p q (a s) -> p q s a", a=2)[:, :, 0:n, :],
                                            AX.X, ALU.add).then_inc(s_read, 1)
                    wait(dve, s_read, c + 1, t, BODY // BLK)
                    nc.vector.tensor_tensor(masked[:, :, 1:n + 1], masked[:, :, 1:n + 1], keep[:, :, bass.ds(s0, n)],
                                            ALU.mult).then_inc(s_soft, 1)
                    wait(dve, s_soft, SOFT * c + 1, t, SOFT * BODY // BLK)
                    nc.vector.tensor_tensor(masked[:, :, 1:n + 1], masked[:, :, 1:n + 1], sunk[:, :, bass.ds(s0, n)],
                                            ALU.add).then_inc(s_soft, 1)
                c = block_at(tau, SOFT_LAG)
                if c is not None:
                    wait(dve, s_soft, SOFT * c + 2, t, SOFT * BODY // BLK)
                    n = steps_of(c) + 1
                    nc.vector.tensor_reduce(new_max[:, :, :], masked[:, :, 0:n], AX.X, ALU.max).then_inc(s_soft, 1)
                c = block_at(tau, SOFT_LAG + 1)
                if c is not None:
                    wait(dve, s_soft, SOFT * c + 3, t, SOFT * BODY // BLK)
                    wait(dve, s_exp, c, t, BODY // BLK)
                    n = steps_of(c) + 1
                    nc.vector.tensor_tensor(shifted[:, :, 0:n], masked[:, :, 0:n],
                                            new_max[:, :, :].to_broadcast([P, Q, n]), ALU.subtract)\
                      .then_inc(s_soft, 1)
                    wait(dve, s_soft, SOFT * c + 4, t, SOFT * BODY // BLK)
                    nc.vector.tensor_copy(masked[:, :, 0:1], new_max[:, :, :]).then_inc(s_soft, 1)
                for q in range(Q):
                    c = block_at(tau, SUM_LAG[q])
                    if c is not None:
                        wait(dve, s_mix, MIX * c + MIX - Q + q + 1, t, MIX * BODY // BLK)
                        n = steps_of(c) + 1
                        nc.vector.tensor_reduce(acc[:, q, :], mix[:, q, 0:n, :].rearrange("p s d -> p d s"), AX.X,
                                                ALU.add).then_inc(s_sum, 1)

            run(dve, slot)
            wait(dve, s_sum, Q * NBLK, 0, 0)
            nc.vector.reciprocal(inv[:, :, :], acc[:, :, D:D + 1]).then_inc(s_fin, 1)
            dve.wait_ge(s_fin, 1)
            nc.vector.tensor_tensor(result[:, :, :], acc[:, :, 0:D], inv[:, :, :].to_broadcast([P, Q, D]), ALU.mult)\
              .then_inc(s_fin, 1)


_INS = ['r_mask', 'L0_rec_sequence_emb', 'L0_rec_target_emb', 'L0_rec_pos_emb', 'L0_rec_proj_w', 'L0_rec_proj_b',
        'L0_rec_w1', 'L0_rec_b1', 'L0_rec_w2', 'L0_rec_b2', 'L0_rec_w3', 'L0_rec_b3']


def kernel(**inputs):
    import numpy as _np
    import concourse.bacc as _bacc
    from concourse import mybir as _mybir
    from concourse.bass_utils import run_bass_kernel_spmd as _run

    nc = _bacc.Bacc("TRN2", target_bir_lowering=False, num_devices=1)
    arrays, args = {}, []
    for name in _INS:
        a = _np.ascontiguousarray(inputs[name])
        arrays[f"in_{name}"] = a
        args.append(nc.dram_tensor(f"in_{name}", a.shape, _mybir.dt.from_np(a.dtype), kind="ExternalInput").ap())
    b, _, d = inputs['L0_rec_sequence_emb'].shape
    out = nc.dram_tensor("out_dram", (b, d), _mybir.dt.float32, kind="ExternalOutput").ap()
    din_attention_program(nc, *args, out)
    r = _run(nc, [arrays], core_ids=[0])
    return r.results[0]["out_dram"]
```

```python
import concourse.bass as bass
from concourse import mybir
from contextlib import ExitStack


def din_attention_program(nc, r_mask, seq, target, pos_emb, proj_w, proj_b, w1, b1, w2, b2, w3, b3, out):
    fp32 = mybir.dt.float32
    fp32r = mybir.dt.float32r
    i32 = mybir.dt.int32
    ALU = mybir.AluOpType
    ACT = mybir.ActivationFunctionType
    AX = mybir.AxisListType

    B, S, D = seq.shape
    H1, H2 = w2.shape
    POS = pos_emb.shape[1]
    P = 128
    Q = B // P
    BLK = 12
    TRI = 3
    K2 = BLK // TRI
    NBLK = -(-S // BLK)
    LASTN = S - (NBLK - 1) * BLK
    NTRI = -(-S // TRI)
    SPAD = NBLK * BLK
    NEG_INF = -1000000000.0
    LOWEST = -3.0e38

    BODY = 4 * BLK
    LOOP0 = 32
    TURNS = (S - LOOP0) // BODY
    LOOP1 = LOOP0 + TURNS * BODY
    END = S + 37
    SEQ_LAG, PROD_LAG, L1_LAG, ADD_LAG, HID_LAG, LO_LAG, L2_LAG, H2_LAG, L3_LAG = 1, 2, 4, 5, 6, 7, 10, 11, 13
    ROWS_LAG, TR_LAG, SOFT_LAG, EXP_LAG = 25, 26, 27, 29
    MIX_LAG = (29, 31, 33, 35)
    VMIX_LAG = 30
    SUM_LAG = (32, 34, 36, 38)
    LAST_SUM_LAG = (31, 32, 33, 34)
    WHOLE = (0, 6)
    SPLITS = BLK - len(WHOLE)
    WMUL_LAG, WADD_LAG = -10, -7
    NCLEAR = 4
    FIRST = 6
    LATE_SLOT = 6
    MASK_SLOT = 14
    NX, NZ, NH, NG = 6, 3, 6, 2
    RING = 4

    seq_v = seq.rearrange("(p q) s d -> p q s d", q=Q)
    mask_v = r_mask.rearrange("(p q) s -> p q s", q=Q)
    tgt_v = target.rearrange("(p q) d -> p q d", q=Q)
    out_v = out.rearrange("(p q) d -> p q d", q=Q)

    ctx = ExitStack()
    with ctx:
        ctx.enter_context(nc.allow_non_contiguous_dma(reason="a few small vectors and the transposed position table"))

        def sb(name, shape, dt=fp32):
            return ctx.enter_context(nc.sbuf_tensor(name, shape, dt))

        def ps(name):
            return ctx.enter_context(nc.psum_tensor(name, [P, 512], fp32))

        def sem(name):
            return ctx.enter_context(nc.semaphore(name))

        seq_sb = [sb(f"seq_sb{r}", [P, Q, BLK, D]) for r in range(RING)]
        mask_i = sb("mask_i", [P, Q, S], i32)
        tgt_sb = sb("tgt_sb", [P, Q, D])
        pos_t = sb("pos_t", [POS, S])
        proj_t2 = sb("proj_t2", [D, 2, D])
        proj_p2 = sb("proj_p2", [POS, 2, D])
        proj_b2 = sb("proj_b2", [P, 1])
        w1_sb = sb("w1_sb", [P, 4, H1])
        w1a, w1b, w1c, w1d = (w1_sb[:, n, :] for n in range(4))
        b1_sb = sb("b1_sb", [H1, 1])
        w2_raw = sb("w2_raw", [H1, H2])
        b2_3 = sb("b2_3", [TRI * H2, 1])
        w3_raw = sb("w3_raw", [H2, 1])
        b3_sb = sb("b3_sb", [BLK, 1])
        ident = sb("ident", [P, P])
        ones = sb("ones", [P, BLK])
        w_add = sb("w_add", [P, 2, H1])
        w_tgt = sb("w_tgt", [P, H1])
        tgt_t = sb("tgt_t", [D, 512])
        T2 = sb("T2", [P, 512])
        P_t = sb("P_t", [D, S])
        w_mul = sb("w_mul", [P, SPAD])
        U = sb("U", [H1, 512])
        V = sb("V", [P, SPAD])
        w2h = sb("w2h", [H1, TRI, H2])
        w2s = sb("w2s", [P, TRI, TRI * H2])
        w2p = sb("w2p", [P, TRI, 2, TRI * H2], fp32r)
        w3s = sb("w3s", [P, K2, BLK])
        w3p = sb("w3p", [P, K2, 2, BLK], fp32r)
        w3h = sb("w3h", [H2, 1])
        bias2 = sb("bias2", [TRI * H2, 1])
        bias3 = sb("bias3", [2 * BLK, 1])
        keep = sb("keep", [P, Q, S])
        sunk = sb("sunk", [P, Q, S])
        W = [sb(f"W{r}", [P, BLK, H1]) for r in range(RING)]
        Vb = [sb(f"Vb{r}", [P, BLK]) for r in range(RING)]
        X = [sb(f"X{r}", [P, 512]) for r in range(NX)]
        Z = [sb(f"Z{r}", [H1, 512]) for r in range(NZ)]
        Hid = [sb(f"Hid{r}", [P, 512]) for r in range(NH)]
        Hhi = [sb(f"Hhi{r}", [P, 512], fp32r) for r in range(NH)]
        Hlo = [sb(f"Hlo{r}", [P, 512], fp32r) for r in range(NH)]
        Ghi = [sb(f"Ghi{r}", [P, 512], fp32r) for r in range(NG)]
        Glo = [sb(f"Glo{r}", [P, 512], fp32r) for r in range(NG)]
        rows = sb("rows", [P, 512])
        masked = sb("masked", [P, Q, BLK + 1])
        shifted = sb("shifted", [P, Q, BLK + 1])
        new_max = sb("new_max", [P, Q, 1])
        E = sb("E", [P, Q, BLK + 1])
        mix = sb("mix", [P, Q, BLK + 1, D + 1])
        acc = sb("acc", [P, Q, D + 1])
        inv = sb("inv", [P, Q, 1])
        result = sb("result", [P, Q, D])

        pT = [ps(f"pT{i}") for i in range(2)]
        pL1 = [ps(f"pL1{i}") for i in range(2)]
        pL2 = [ps(f"pL2{i}") for i in range(2)]
        pL3 = ps("pL3")
        pSc = ps("pSc")

        s_seq = [sem(f"seq_loaded{r}") for r in range(RING)]
        s_seq0 = sem("first_steps_loaded")
        s_tgt = sem("target_loaded")
        s_proj = sem("projection_loaded")
        s_w1 = sem("w1_loaded")
        s_small = sem("first_biases_loaded")
        s_w2 = sem("w2_loaded")
        s_late = sem("w3_and_biases_loaded")
        s_mask = sem("mask_loaded")
        s_keep = sem("mask_factors")
        s_zero = sem("w3_cleared")
        s_clear = sem("hidden_cleared")
        s_set = sem("gpsimd_setup")
        s_pset = sem("tensor_setup")
        s_vset = sem("vector_setup")
        s_aset = sem("scalar_setup")
        s_tr = sem("pair_transposed")
        s_copy = sem("seq_copied")
        s_prod = sem("product_written")
        s_wp = sem("split_step")
        s_w = sem("weights_built")
        s_wstep = sem("weights_step")
        s_l1 = sem("layer1_done")
        s_add = sem("targets_added")
        s_hid = sem("hidden1_done")
        s_lo = sem("hidden1_split")
        s_l2 = sem("layer2_done")
        s_g = sem("hidden2_done")
        s_glo = sem("hidden2_split")
        s_l3 = sem("layer3_done")
        s_rows = sem("rows_copied")
        s_sc = sem("scores_transposed")
        s_read = sem("scores_read")
        s_soft = sem("softmax_step")
        s_exp = sem("exp_done")
        s_mix = sem("mix_done")
        s_vmix = sem("mix_done_by_vector")
        s_sum = sem("block_summed")
        s_fin = sem("final_step")
        s_out = sem("output_stored")

        SOFT = 5
        WSTEP = 2
        MIX = len(MIX_LAG)
        VMIX = 2 + Q - MIX

        FROM_1 = {"scalar": (s_hid, s_exp), "tensor": (s_l1, s_sc), "gpsimd": (s_mix,),
                  "vector": (s_read, s_sum, s_vmix)}

        def start_from_1(eng, name):
            for s in FROM_1[name]:
                eng.sem_inc(s, 1)

        def base(s):
            return 1 if any(s is x for group in FROM_1.values() for x in group) else 0

        def wait(eng, s, first, t, per_turn):
            if isinstance(t, int):
                if first > 0:
                    eng.wait_ge(s, base(s) + first)
            else:
                assert base(s) + first > 0
                eng.wait_ge(s, t * per_turn + (base(s) + first))

        def run(eng, slot, first=0):
            for tau in range(first, LOOP0):
                slot(tau, 0)
            with eng.Fori(0, TURNS) as t:
                for tau in range(LOOP0, LOOP0 + BODY):
                    slot(tau, t)
            for tau in range(LOOP1, END):
                slot(tau, 0)

        def block_at(tau, lag):
            c, r = divmod(tau - lag, BLK)
            return c if r == 0 and 0 <= c < NBLK else None

        def is_split(g):
            return g % BLK not in WHOLE and g < S - 2

        def splits_before(g):
            return sum(is_split(i) for i in range(g))

        def block_to_sum(tau, q):
            c, last = block_at(tau, SUM_LAG[q]), block_at(tau, LAST_SUM_LAG[q])
            if last is not None and last >= NBLK - 2:
                return last
            return c if c is not None and c < NBLK - 2 else None

        def pool_batches(c):
            return Q // 2 if c == NBLK - 1 else MIX

        def steps_of(c):
            return LASTN if c == NBLK - 1 else BLK

        N_PROJ, N_W1, N_SMALL, N_LATE = 3, 2, 3, 2 * TRI + 2

        block = ctx.enter_context(nc.Block())

        @block.sync
        def _(sp):
            sp.dma_start(tgt_sb[:, :, :], tgt_v).then_inc(s_tgt, 16)
            sp.dma_start(proj_t2[:, :, :], proj_w[0:D, :].unsqueeze(1).to_broadcast([D, 2, D])).then_inc(s_proj, 16)
            sp.dma_start(w1_sb[0:D, :, :], w1.rearrange("(n d) h -> d n h", d=D)).then_inc(s_w1, 16)
            for h in range(2):
                sp.dma_start(proj_b2[h * D:(h + 1) * D, :], proj_b.rearrange("(d a) -> d a", a=1))\
                  .then_inc(s_small, 16)
            sp.dma_start(b1_sb[:, :], b1.rearrange("(h a) -> h a", a=1)).then_inc(s_small, 16)
            sp.dma_start(w2_raw[:, :], w2).then_inc(s_w2, 16)
            sp.dma_start(w3_raw[:, :], w3).then_inc(s_late, 16)
            sp.dma_start(seq_sb[0][:, :, FIRST:BLK, :], seq_v[:, :, FIRST:BLK, :]).then_inc(s_seq[0], 16)
            sp.wait_ge(s_zero, 1)
            for g in range(TRI):
                sp.dma_start(w3s[g * H2:(g + 1) * H2, :, :].rearrange("h k c -> h (k c)")[:, g::BLK + TRI],
                             w3.to_broadcast([H2, K2])).then_inc(s_late, 16)
            for g in range(TRI):
                sp.dma_start(b2_3[g * H2:(g + 1) * H2, :], b2.rearrange("(h a) -> h a", a=1)).then_inc(s_late, 16)
            sp.dma_start(b3_sb[:, :], b3.rearrange("(a b) -> a b", a=1).to_broadcast([BLK, 1])).then_inc(s_late, 16)
            sp.dma_start(mask_i[:, :, :], mask_v).then_inc(s_mask, 16)
            for c in range(1, RING):
                sp.dma_start(seq_sb[c][:, :, :, :], seq_v[:, :, c * BLK:(c + 1) * BLK, :]).then_inc(s_seq[c], 16)
            for c in range(RING, NBLK):
                wait(sp, s_mix, MIX * (c - RING + 1), 0, 0)
                wait(sp, s_vmix, VMIX * (c - RING + 1), 0, 0)
                n = steps_of(c)
                sp.dma_start(seq_sb[c % RING][:, :, 0:n, :], seq_v[:, :, c * BLK:c * BLK + n, :])\
                  .then_inc(s_seq[c % RING], 16)
            sp.wait_ge(s_fin, 2)
            sp.dma_start(out_v, result[:, :, :]).then_inc(s_out, 16)
            sp.wait_ge(s_out, 16)

        @block.scalar
        def _(act):
            start_from_1(act, "scalar")
            act.dma_start(proj_p2[:, :, :], proj_w[D:D + POS, :].unsqueeze(1).to_broadcast([POS, 2, D]))\
               .then_inc(s_proj, 16)
            act.dma_start(pos_t[:, :], pos_emb.rearrange("s j -> j s")).then_inc(s_proj, 16)
            act.dma_start(w1_sb[D:2 * D, :, :], w1.rearrange("(n d) h -> d n h", d=D)).then_inc(s_w1, 16)
            act.dma_start(seq_sb[0][:, :, 0:FIRST, :], seq_v[:, :, 0:FIRST, :]).then_inc(s_seq0, 16)
            act.wait_ge(s_clear, 1)
            for part in Hhi[:NH // 2]:
                nc.scalar.activation(part[:, :], Hid[0][:, :], ACT.Copy)
            act.wait_ge(s_pset, 3)
            act.wait_ge(s_small, 16 * N_SMALL)
            nc.scalar.activation(T2[:, :], pL1[1][:, :], ACT.Identity, bias=proj_b2[:, 0:1]).then_inc(s_aset, 1)

            def slot(tau, t):
                g = tau - SEQ_LAG
                if 0 <= g < S:
                    h = g % 2 * D
                    if g % 2 == 0:
                        wait(act, s_tr, g // 2 + 1, t, BODY // 2)
                    wait(act, s_l1, g - NX + 1, t, BODY)
                    nc.scalar.activation(X[g % NX][h:h + D, :], pT[g // 2 % 2][h:h + D, :], ACT.Copy)\
                      .then_inc(s_copy, 1)
                g = tau - HID_LAG
                if 0 <= g < S:
                    wait(act, s_add, g + 1, t, BODY)
                    wait(act, s_l2, g - NH + 1, t, BODY)
                    for part in (Hid, Hhi) if is_split(g) else (Hid,):
                        last = nc.scalar.activation(part[g % NH][0:H1, :], Z[g % NZ][:, :], ACT.Tanh, scale=0.5)
                    last.then_inc(s_hid, 1)
                g = tau - H2_LAG
                if 0 <= g < S and (g % TRI == TRI - 1 or g == S - 1):
                    k = g // TRI
                    wait(act, s_l2, g + 1, t, BODY)
                    wait(act, s_l3, k - NG + 1, t, BODY // TRI)
                    for part in (Ghi[k % NG], pL2[k % 2]):
                        last = nc.scalar.activation(part[0:TRI * H2, :], pL2[k % 2][0:TRI * H2, :], ACT.Tanh,
                                                    scale=0.5, bias=bias2[:, 0:1])
                    last.then_inc(s_g, 1)
                c = block_at(tau, ROWS_LAG)
                if c is not None:
                    wait(act, s_l3, min(K2 * (c + 1), NTRI), t, BODY // TRI)
                    wait(act, s_sc, c, t, BODY // BLK)
                    nc.scalar.activation(rows[0:2 * BLK, :], pL3[0:2 * BLK, :], ACT.Identity, bias=bias3[:, 0:1])\
                      .then_inc(s_rows, 1)
                c = block_at(tau, EXP_LAG)
                if c is not None:
                    wait(act, s_soft, SOFT * c + 4, t, SOFT * BODY // BLK)
                    wait(act, s_mix, MIX * c, t, MIX * BODY // BLK)
                    wait(act, s_vmix, VMIX * c, t, VMIX * BODY // BLK)
                    n = steps_of(c) + 1
                    nc.scalar.activation(E[:, :, 0:n], shifted[:, :, 0:n], ACT.Exp).then_inc(s_exp, 1)

            for tau in range(L1_LAG):
                slot(tau, 0)
            for part in Hhi[NH // 2:]:
                nc.scalar.activation(part[:, :], Hid[0][:, :], ACT.Copy)
            for tau in range(L1_LAG, HID_LAG):
                slot(tau, 0)
            act.wait_ge(s_clear, 2)
            act.wait_ge(s_set, 3)
            for tau in range(HID_LAG, H2_LAG):
                slot(tau, 0)
            act.wait_ge(s_vset, 8)
            run(act, slot, H2_LAG)

        @block.tensor
        def _(pe):
            start_from_1(pe, "tensor")
            pe.wait_ge(s_tgt, 16)
            pe.wait_ge(s_set, 2)
            for q in range(Q):
                last = nc.tensor.transpose(pL1[0][0:D, q * P:(q + 1) * P], tgt_sb[:, q, :], ident[:, :])
            last.then_inc(s_pset, 1)
            pe.wait_ge(s_proj, 16 * N_PROJ)
            nc.tensor.matmul(pL2[0][:, 0:S], proj_p2[:, :, :].rearrange("k a m -> k (a m)"), pos_t[:, :],
                             start=True, stop=True).then_inc(s_pset, 1)
            pe.wait_ge(s_vset, 2)
            nc.tensor.matmul(pL1[1][:, :], proj_t2[:, :, :].rearrange("k a m -> k (a m)"), tgt_t[:, :],
                             start=True, stop=True).then_inc(s_pset, 1)
            pe.wait_ge(s_vset, 3)
            nc.tensor.matmul(pL2[1][0:H1, 0:S], w_tgt[0:D, :], P_t[:, :], start=True, stop=True).then_inc(s_pset, 1)

            def slot(tau, t):
                if tau == LATE_SLOT + 1:
                    pe.wait_ge(s_vset, 7)
                    nc.tensor.matmul(pL3[0:TRI * H2, 0:1], w2h[:, :, :].rearrange("k a m -> k (a m)"), ones[0:H1, 0:1],
                                     start=True, stop=True).then_inc(s_pset, 1)
                    nc.tensor.matmul(pSc[0:BLK, 0:1], ones[0:H2, :], w3h[:, :], start=True, stop=True)\
                      .then_inc(s_pset, 1)
                if tau % 2 == 0 and tau < S:
                    p, c, i = tau // 2, tau // BLK, tau % BLK
                    if tau == 0:
                        pe.wait_ge(s_seq0, 16)
                    if i == (FIRST if c == 0 and isinstance(t, int) else 0):
                        wait(pe, s_seq[c % RING], 16 * (c // RING + 1), t, 16)
                    wait(pe, s_prod, 2 * (p - 2) + 2, t, BODY)
                    for q in range(Q):
                        last = nc.tensor.transpose(
                            pT[p % 2][:, q * P:(q + 1) * P],
                            seq_sb[c % RING][:, q, i:i + 2, :].rearrange("p s d -> p (s d)"), ident[:, :])
                    last.then_inc(s_tr, 1)
                g = tau - L2_LAG
                if 0 <= g < S:
                    k, j = divmod(g, TRI)
                    if is_split(g):
                        wait(pe, s_lo, splits_before(g) + 1, t, SPLITS * BODY // BLK)
                    else:
                        wait(pe, s_hid, g + 1, t, BODY)
                    if j == 0:
                        wait(pe, s_glo, k - 1, t, BODY // TRI)
                    r = g % NH
                    parts = [(w2s[:, j, :], Hid[r])] if not is_split(g) else \
                        [(w2p[:, j, 0, :], Hhi[r]), (w2p[:, j, 1, :], Hhi[r]), (w2p[:, j, 0, :], Hlo[r])]
                    for n, (w, hid) in enumerate(parts):
                        last = nc.tensor.matmul(pL2[k % 2][0:TRI * H2, :], w, hid[:, :],
                                                start=(j == 0 and n == 0),
                                                stop=((j == TRI - 1 or g == S - 1) and n == len(parts) - 1))
                    last.then_inc(s_l2, 1)
                g = tau - L1_LAG
                if 0 <= g < S:
                    if g % BLK == 0:
                        wait(pe, s_w, g // BLK + 1, t, BODY // BLK)
                    wait(pe, s_prod, g + 1, t, BODY)
                    wait(pe, s_add, g - 1, t, BODY)
                    nc.tensor.matmul(pL1[g % 2][0:H1, :], W[g // BLK % RING][:, g % BLK, :], X[g % NX][:, :],
                                     start=True, stop=True).then_inc(s_l1, 1)
                g = tau - L3_LAG
                if 0 <= g < S and (g % TRI == TRI - 1 or g == S - 1):
                    k = g // TRI
                    j = k % K2
                    wait(pe, s_glo, k + 1, t, BODY // TRI)
                    if j == 0:
                        wait(pe, s_rows, k // K2, t, BODY // BLK)
                    w = w3p[:, j, :, :].rearrange("k a m -> k (a m)")
                    nc.tensor.matmul(pL3[0:2 * BLK, :], w, Ghi[k % NG][:, :], start=(j == 0), stop=False)
                    nc.tensor.matmul(pL3[0:2 * BLK, :], w, Glo[k % NG][:, :], start=False,
                                     stop=(j == K2 - 1 or g == S - 1)).then_inc(s_l3, 1)
                c = block_at(tau, TR_LAG)
                if c is not None:
                    wait(pe, s_rows, c + 1, t, BODY // BLK)
                    wait(pe, s_read, c, t, BODY // BLK)
                    for q in range(Q):
                        last = nc.tensor.transpose(pSc[:, q * P:(q + 1) * P], rows[:, q * P:(q + 1) * P], ident[:, :])
                    last.then_inc(s_sc, 1)

            for tau in range(4):
                slot(tau, 0)
            pe.wait_ge(s_aset, 1)
            pe.wait_ge(s_vset, 4)
            nc.tensor.matmul(pL2[0][0:H1, :], w_tgt[0:D, :], T2[0:D, :], start=True, stop=True).then_inc(s_pset, 1)
            run(pe, slot, 4)

        @block.gpsimd
        def _(pool):
            start_from_1(pool, "gpsimd")
            nc.gpsimd.memset(ident[:, :], 0.0).then_inc(s_set, 1)
            nc.gpsimd.memset(ones[:, :], 1.0)
            pool.wait_ge(s_set, 1)
            nc.gpsimd.affine_select(out=ident[:, :], in_=ident[:, :], compare_op=ALU.not_equal, fill=1.0, base=0,
                                    pattern=[[-1, P]], channel_multiplier=1).then_inc(s_set, 1)
            nc.gpsimd.memset(acc[:, :, :], 0.0)
            nc.gpsimd.memset(rows[:, :], 0.0)
            for part in Hid[NCLEAR:]:
                nc.gpsimd.memset(part[:, :], 0.0)
            for part in Ghi + Glo:
                last = nc.gpsimd.memset(part[:, :].bitcast(fp32), 0.0)
            last.then_inc(s_set, 1)

            def weights_mul(c, t):
                r = c % RING
                s0 = c * BLK if isinstance(t, int) else t * BODY + c * BLK
                if c == 0:
                    pool.wait_ge(s_vset, 4)
                wait(pool, s_l1, BLK * (c - RING + 1), t, BODY)
                nc.gpsimd.tensor_tensor(W[r][:, :, :],
                                        w_mul[:, bass.ds(s0, BLK)].unsqueeze(2).to_broadcast([P, BLK, H1]),
                                        w1d[:, :].unsqueeze(1).to_broadcast([P, BLK, H1]), ALU.mult)\
                  .then_inc(s_wstep, 1)
                if c == 0:
                    pool.wait_ge(s_vset, 5)
                wait(pool, s_add, BLK * (c - RING + 1), t, BODY)
                nc.gpsimd.tensor_copy(Vb[r][:, :], V[:, bass.ds(s0, BLK)]).then_inc(s_wstep, 1)

            def weights_add(c, t):
                wait(pool, s_wstep, WSTEP * (c + 1), t, WSTEP * BODY // BLK)
                pairs = W[c % RING][:, :, :].rearrange("p (s e) h -> p s e h", e=2)
                nc.gpsimd.tensor_tensor(pairs, pairs, w_add[:, :, :].unsqueeze(1).to_broadcast([P, BLK // 2, 2, H1]),
                                        ALU.add).then_inc(s_w, 1)

            for c in range(2):
                weights_mul(c, 0)
                weights_add(c, 0)

            def slot(tau, t):
                g = tau - LO_LAG
                if 0 <= g < S and is_split(g):
                    wait(pool, s_hid, g + 1, t, BODY)
                    wait(pool, s_l2, g - NH + 1, t, BODY)
                    nc.gpsimd.tensor_tensor(Hlo[g % NH][:, :], Hid[g % NH][:, :], Hhi[g % NH][:, :].bitcast(fp32),
                                            ALU.subtract).then_inc(s_lo, 1)
                c = block_at(tau, WMUL_LAG)
                if c is not None and c >= 2:
                    weights_mul(c, t)
                c = block_at(tau, WADD_LAG)
                if c is not None and c >= 2:
                    weights_add(c, t)
                for q in range(MIX):
                    c = block_at(tau, MIX_LAG[q])
                    if c is not None and q < pool_batches(c):
                        n = steps_of(c)
                        wait(pool, s_exp, c + 1, t, BODY // BLK)
                        wait(pool, s_sum, Q * c, t, Q * BODY // BLK)
                        nc.gpsimd.tensor_tensor(mix[:, q, 1:n + 1, 0:D], seq_sb[c % RING][:, q, 0:n, :],
                                                E[:, q, 1:n + 1].unsqueeze(2).to_broadcast([P, n, D]), ALU.mult)\
                          .then_inc(s_mix, 1)

            run(pool, slot)

        @block.vector
        def _(dve):
            start_from_1(dve, "vector")
            nc.vector.memset(w3s[:, :, :], 0.0).then_inc(s_zero, 1)
            nc.vector.memset(Hid[0][:, :], 0.0).then_inc(s_clear, 1)
            nc.vector.memset(w_add[:, :, :], 0.0)
            nc.vector.memset(w_mul[:, :], 1.0)
            nc.vector.memset(V[:, :], 0.0)
            nc.vector.memset(bias3[:, :], 0.0)
            nc.vector.memset(masked[:, :, 0:1], LOWEST)
            nc.vector.memset(w2s[:, :, :], 0.0).then_inc(s_vset, 1)
            for hid in Hid[1:NCLEAR]:
                last = nc.vector.memset(hid[:, :], 0.0)
            last.then_inc(s_clear, 1)
            dve.wait_ge(s_pset, 1)
            nc.vector.tensor_copy(tgt_t[:, :], pL1[0][0:D, :]).then_inc(s_vset, 1)
            dve.wait_ge(s_pset, 2)
            nc.vector.tensor_copy(P_t[:, :], pL2[0][0:D, 0:S])
            dve.wait_ge(s_w1, 16 * N_W1)
            nc.vector.tensor_tensor(w_tgt[:, :], w1a, w1c, ALU.add).then_inc(s_vset, 1)
            dve.wait_ge(s_vset, 1)
            for h in range(2):
                half = slice(h * D, (h + 1) * D)
                nc.vector.tensor_tensor(w_add[half, h, :], w1b[half, :], w1c[half, :], ALU.subtract)
                last = nc.vector.tensor_copy(w_mul[half, h:S:2], pL2[0][half, h:S:2])
            last.then_inc(s_vset, 1)
            dve.wait_ge(s_pset, 4)
            dve.wait_ge(s_small, 16 * N_SMALL)
            nc.vector.tensor_scalar(V[0:H1, 0:S], pL2[1][0:H1, 0:S], b1_sb[:, 0:1], None, ALU.add)\
              .then_inc(s_vset, 1)
            dve.wait_ge(s_w2, 16)
            nc.vector.tensor_scalar(w2h[:, :, :], w2_raw[:, :].unsqueeze(1).to_broadcast([H1, TRI, H2]), 0.5, None,
                                    ALU.mult)
            for g in range(TRI):
                last = nc.vector.tensor_scalar(w2s[0:H1, g, g * H2:(g + 1) * H2], w2_raw[:, :], 0.5, None, ALU.mult)
            last.then_inc(s_wp, 1)
            dve.wait_ge(s_wp, 1)
            nc.vector.tensor_copy(w2p[:, :, 0, :], w2s[:, :, :]).then_inc(s_wp, 1)
            dve.wait_ge(s_wp, 2)
            nc.vector.tensor_tensor(w2p[:, :, 1, :], w2s[:, :, :], w2p[:, :, 0, :].bitcast(fp32), ALU.subtract)

            def later_layers():
                dve.wait_ge(s_late, 16 * N_LATE)
                nc.vector.tensor_scalar(w3h[:, :], w3_raw[:, :], 0.5, None, ALU.mult)
                nc.vector.tensor_scalar(w3p[:, :, 0, :], w3s[:, :, :], 0.5, None, ALU.mult).then_inc(s_wp, 1)
                dve.wait_ge(s_wp, 3)
                nc.vector.scalar_tensor_tensor(out=w3p[:, :, 1, :], in0=w3s[:, :, :], scalar=0.5,
                                               in1=w3p[:, :, 0, :].bitcast(fp32), op0=ALU.mult, op1=ALU.subtract)\
                  .then_inc(s_vset, 1)

            def later_biases():
                dve.wait_ge(s_pset, 7)
                nc.vector.tensor_scalar(bias2[:, :], pL3[0:TRI * H2, 0:1], b2_3[:, 0:1], 0.5, ALU.add, ALU.mult)
                nc.vector.tensor_tensor(bias3[0:BLK, :], pSc[0:BLK, 0:1], b3_sb[:, :], ALU.add).then_inc(s_vset, 1)

            def mask_factors():
                dve.wait_ge(s_mask, 16)
                nc.vector.tensor_scalar(keep[:, :, :], mask_i[:, :, :], 0.0, None, ALU.not_equal).then_inc(s_keep, 1)
                dve.wait_ge(s_keep, 1)
                nc.vector.tensor_scalar(sunk[:, :, :], keep[:, :, :], 1.0, -NEG_INF, ALU.subtract, ALU.mult)\
                  .then_inc(s_keep, 1)

            def add_parts(c, t):
                n = steps_of(c)
                wait(dve, s_sc, c + 1, t, BODY // BLK)
                nc.vector.tensor_reduce(masked[:, :, 1:n + 1], pSc[:, :].rearrange("p (q s) -> p q s", q=Q)
                                        [:, :, 0:2 * BLK].rearrange("p q (a s) -> p q s a", a=2)[:, :, 0:n, :],
                                        AX.X, ALU.add).then_inc(s_read, 1)

            def mask_scores(c, t):
                n = steps_of(c)
                s0 = c * BLK if isinstance(t, int) else t * BODY + c * BLK
                wait(dve, s_read, c + 1, t, BODY // BLK)
                nc.vector.tensor_tensor(masked[:, :, 1:n + 1], masked[:, :, 1:n + 1], keep[:, :, bass.ds(s0, n)],
                                        ALU.mult).then_inc(s_soft, 1)

            def sink_masked(c, t):
                n = steps_of(c)
                s0 = c * BLK if isinstance(t, int) else t * BODY + c * BLK
                wait(dve, s_soft, SOFT * c + 1, t, SOFT * BODY // BLK)
                nc.vector.tensor_tensor(masked[:, :, 1:n + 1], masked[:, :, 1:n + 1], sunk[:, :, bass.ds(s0, n)],
                                        ALU.add).then_inc(s_soft, 1)

            def find_max(c, t):
                wait(dve, s_soft, SOFT * c + 2, t, SOFT * BODY // BLK)
                nc.vector.tensor_reduce(new_max[:, :, :], masked[:, :, 0:steps_of(c) + 1], AX.X, ALU.max)\
                  .then_inc(s_soft, 1)

            def take_max_off(c, t):
                wait(dve, s_soft, SOFT * c + 3, t, SOFT * BODY // BLK)
                wait(dve, s_exp, c, t, BODY // BLK)
                n = steps_of(c) + 1
                nc.vector.tensor_tensor(shifted[:, :, 0:n], masked[:, :, 0:n],
                                        new_max[:, :, :].to_broadcast([P, Q, n]), ALU.subtract).then_inc(s_soft, 1)

            def carry_max(c, t):
                wait(dve, s_soft, SOFT * c + 4, t, SOFT * BODY // BLK)
                nc.vector.tensor_copy(masked[:, :, 0:1], new_max[:, :, :]).then_inc(s_soft, 1)

            def small_step(step, tau, lag, t):
                c = block_at(tau, lag)
                if c is not None:
                    step(c, t)

            def slot(tau, t):
                if tau == ADD_LAG - 1:
                    dve.wait_ge(s_pset, 5)
                    nc.vector.tensor_copy(U[:, :], pL2[0][0:H1, :]).then_inc(s_vset, 1)
                    dve.wait_ge(s_vset, 6)
                if tau == LATE_SLOT:
                    later_layers()
                if tau == LATE_SLOT + 2:
                    later_biases()
                if tau == MASK_SLOT:
                    mask_factors()
                small_step(find_max, tau, SOFT_LAG + 1, t)
                g = tau - PROD_LAG
                if 0 <= g < S:
                    h = g % 2 * D
                    wait(dve, s_copy, g + 1, t, BODY)
                    nc.vector.tensor_tensor(X[g % NX][D - h:P - h, :], pT[g // 2 % 2][h:h + D, :], T2[h:h + D, :],
                                            ALU.mult).then_inc(s_prod, 1)
                small_step(add_parts, tau, SOFT_LAG, t)
                small_step(take_max_off, tau, SOFT_LAG + 1, t)
                g = tau - ADD_LAG
                if 0 <= g < S:
                    wait(dve, s_l1, g + 1, t, BODY)
                    wait(dve, s_hid, g - NZ + 1, t, BODY)
                    if g % BLK == 0:
                        wait(dve, s_w, g // BLK + 1, t, BODY // BLK)
                    nc.vector.scalar_tensor_tensor(out=Z[g % NZ][:, :], in0=pL1[g % 2][0:H1, :],
                                                   scalar=Vb[g // BLK % RING][0:H1, g % BLK:g % BLK + 1],
                                                   in1=U[:, :], op0=ALU.add, op1=ALU.add).then_inc(s_add, 1)
                small_step(mask_scores, tau, SOFT_LAG, t)
                small_step(carry_max, tau, SOFT_LAG + 1, t)
                g = tau - H2_LAG - 1
                if 0 <= g < S and (g % TRI == TRI - 1 or g == S - 1):
                    k = g // TRI
                    wait(dve, s_g, k + 1, t, BODY // TRI)
                    wait(dve, s_l3, k - NG + 1, t, BODY // TRI)
                    nc.vector.tensor_tensor(Glo[k % NG][0:TRI * H2, :], pL2[k % 2][0:TRI * H2, :],
                                            Ghi[k % NG][0:TRI * H2, :].bitcast(fp32), ALU.subtract).then_inc(s_glo, 1)
                small_step(sink_masked, tau, SOFT_LAG, t)
                c = block_at(tau, VMIX_LAG)
                if c is not None:
                    n = steps_of(c)
                    wait(dve, s_exp, c + 1, t, BODY // BLK)
                    wait(dve, s_sum, Q * c, t, Q * BODY // BLK)
                    nc.vector.tensor_tensor(mix[:, :, 0, :], acc[:, :, :], E[:, :, 0:1].to_broadcast([P, Q, D + 1]),
                                            ALU.mult).then_inc(s_vmix, 1)
                    nc.vector.tensor_copy(mix[:, :, 1:n + 1, D], E[:, :, 1:n + 1]).then_inc(s_vmix, 1)
                    for q in range(pool_batches(c), Q):
                        nc.vector.tensor_tensor(mix[:, q, 1:n + 1, 0:D], seq_sb[c % RING][:, q, 0:n, :],
                                                E[:, q, 1:n + 1].unsqueeze(2).to_broadcast([P, n, D]), ALU.mult)\
                          .then_inc(s_vmix, 1)
                for q in range(Q):
                    c = block_to_sum(tau, q)
                    if c is not None:
                        n = steps_of(c) + 1
                        wait(dve, s_vmix, VMIX * (c + 1) + MIX - pool_batches(c), t, VMIX * BODY // BLK)
                        if q < pool_batches(c):
                            wait(dve, s_mix, MIX * c + q + 1, t, MIX * BODY // BLK)
                        nc.vector.tensor_reduce(acc[:, q, :], mix[:, q, 0:n, :].rearrange("p s d -> p d s"), AX.X,
                                                ALU.add).then_inc(s_sum, 1)

            dve.wait_ge(s_aset, 1)
            run(dve, slot)
            wait(dve, s_sum, Q * NBLK, 0, 0)
            nc.vector.reciprocal(inv[:, :, :], acc[:, :, D:D + 1]).then_inc(s_fin, 1)
            dve.wait_ge(s_fin, 1)
            nc.vector.tensor_tensor(result[:, :, :], acc[:, :, 0:D], inv[:, :, :].to_broadcast([P, Q, D]), ALU.mult)\
              .then_inc(s_fin, 1)


_INS = ['r_mask', 'L0_rec_sequence_emb', 'L0_rec_target_emb', 'L0_rec_pos_emb', 'L0_rec_proj_w', 'L0_rec_proj_b',
        'L0_rec_w1', 'L0_rec_b1', 'L0_rec_w2', 'L0_rec_b2', 'L0_rec_w3', 'L0_rec_b3']


def kernel(**inputs):
    import numpy as _np
    import concourse.bacc as _bacc
    from concourse import mybir as _mybir
    from concourse.bass_utils import run_bass_kernel_spmd as _run

    nc = _bacc.Bacc("TRN2", target_bir_lowering=False, num_devices=1)
    arrays, args = {}, []
    for name in _INS:
        a = _np.ascontiguousarray(inputs[name])
        arrays[f"in_{name}"] = a
        args.append(nc.dram_tensor(f"in_{name}", a.shape, _mybir.dt.from_np(a.dtype), kind="ExternalInput").ap())
    b, _, d = inputs['L0_rec_sequence_emb'].shape
    out = nc.dram_tensor("out_dram", (b, d), _mybir.dt.float32, kind="ExternalOutput").ap()
    din_attention_program(nc, *args, out)
    r = _run(nc, [arrays], core_ids=[0])
    return r.results[0]["out_dram"]
```
